# Optimizing a Trainium2 kernel written in Bass

```python
import numpy as np
import jax
import jax.numpy as jnp

def _softmax(x, axis=-1):
    return jax.nn.softmax(x, axis=axis)

def _gelu(x):
    return jax.nn.gelu(x, approximate=True)

def _silu(x):
    return jax.nn.silu(x)

def _sigmoid(x):
    return jax.nn.sigmoid(x)

def _layernorm(x, axis=-1, eps=1e-05):
    m = jnp.mean(x, axis=axis, keepdims=True)
    v = jnp.var(x, axis=axis, keepdims=True)
    return (x - m) / jnp.sqrt(v + eps)

def _scatter_add(tgt, idx, src, axis=0):
    return tgt.at[idx].add(src)

def _segment_sum(src, seg, n):
    return jax.ops.segment_sum(src, seg, n)
kernel_name = 'mk_gps_d2_gnn_r8_052da7'

def setup_inputs(seed: int=0):
    np.random.seed(seed)
    _w = jnp.asarray

    def _rec_inputs():
        import jax
        import jax.numpy as jnp
        _gk = jax.random.key(seed)
        x = -0.0003713 + 1 * jax.random.normal(jax.random.fold_in(_gk, 1), (6250, 256), jnp.float32)
        src = jax.random.randint(jax.random.fold_in(_gk, 2), (200000,), 0, 6250, jnp.int32)
        dst = jax.random.randint(jax.random.fold_in(_gk, 3), (200000,), 0, 6250, jnp.int32)
        _o = jnp.argsort(dst, stable=True)
        src = src[_o]
        dst = dst[_o]
        edge_type_8 = jax.random.randint(jax.random.fold_in(_gk, 12), (200000,), 0, 8, jnp.int32)
        return (x, src, dst, edge_type_8)
    x, src, dst, edge_type_8 = _rec_inputs()

    def _L0_gnn_setup():
        import jax, jax.numpy as jnp
        import numpy as np
        N, E, FIN, H, FO = (6250, 100000, 256, 8, 32)
        key = jax.random.key(seed)
        ks = jax.random.split(key, 7)
        node_features = jax.random.normal(ks[0], (N, FIN), dtype=jnp.float32)
        edge_index = jax.random.randint(ks[1], (2, E), 0, N, dtype=jnp.int32).astype(jnp.int64)
        Wp = jax.random.normal(ks[2], (H * FO, FIN), dtype=jnp.float32) * (1.0 / np.sqrt(FIN))
        a_src = jax.random.normal(ks[3], (1, H, FO), dtype=jnp.float32) * 0.1
        a_trg = jax.random.normal(ks[4], (1, H, FO), dtype=jnp.float32) * 0.1
        Wskip = jax.random.normal(ks[5], (H * FO, FIN), dtype=jnp.float32) * (1.0 / np.sqrt(FIN))
        bias = jnp.zeros((H * FO,), dtype=jnp.float32)
        return {'node_features': node_features, 'edge_index': edge_index, 'Wp': Wp, 'a_src': a_src, 'a_trg': a_trg, 'Wskip': Wskip, 'bias': bias}
    _L0_gnn_all = _L0_gnn_setup()
    _L0_gnn_in = {k: v for k, v in _L0_gnn_all.items() if k in ('Wp', 'a_src', 'a_trg', 'Wskip', 'bias')}
    del _L0_gnn_all

    def _L0_mix_setup():
        import jax, jax.numpy as jnp
        import numpy as np
        NHEAD = 8
        ATT_EPS = 1e-06
        LN_EPS = 1e-05

        def _layernorm(x, g, b):
            mu = jnp.mean(x, axis=-1, keepdims=True)
            var = jnp.mean(jnp.square(x - mu), axis=-1, keepdims=True)
            return (x - mu) * jax.lax.rsqrt(var + LN_EPS) * g + b
        key = jax.random.key(seed)
        ks = jax.random.split(key, 7)
        N, L, C = (4, 2048, 256)
        s = 1.0 / np.sqrt(C)
        return {'x': jax.random.normal(ks[0], (N, L, C), jnp.float32), 'Wq': jax.random.normal(ks[1], (C, C), jnp.float32) * s, 'Wk': jax.random.normal(ks[2], (C, C), jnp.float32) * s, 'Wv': jax.random.normal(ks[3], (C, C), jnp.float32) * s, 'Wm': jax.random.normal(ks[4], (C, C), jnp.float32) * s, 'W1': jax.random.normal(ks[5], (2 * C, 2 * C), jnp.float32) * (1.0 / np.sqrt(2 * C)), 'W2': jax.random.normal(ks[6], (2 * C, C), jnp.float32) * (1.0 / np.sqrt(2 * C)), 'g1': jnp.ones((C,), jnp.float32), 'b1': jnp.zeros((C,), jnp.float32), 'g2': jnp.ones((C,), jnp.float32), 'b2': jnp.zeros((C,), jnp.float32)}
    _L0_mix_all = _L0_mix_setup()
    _L0_mix_in = {k: v for k, v in _L0_mix_all.items() if k in ('Wq', 'Wk', 'Wv', 'Wm', 'W1', 'W2', 'g1', 'b1', 'g2', 'b2')}
    del _L0_mix_all

    def _L0_ffn_setup():
        import jax, jax.numpy as jnp
        import numpy as np
        DIM = 256
        H = 8
        D = 64
        G = 64
        INNER = H * D
        SCALE = D ** (-0.5)
        key = jax.random.key(seed)
        ks = jax.random.split(key, 12)
        B, N = (4, 2048)
        x = jax.random.normal(ks[0], (B, N, DIM), dtype=jnp.float32)
        s = lambda fan_in: 1.0 / np.sqrt(fan_in)
        W_fx = jax.random.normal(ks[1], (DIM, INNER), dtype=jnp.float32) * s(DIM)
        b_fx = jnp.zeros((INNER,), dtype=jnp.float32)
        W_x = jax.random.normal(ks[2], (DIM, INNER), dtype=jnp.float32) * s(DIM)
        b_x = jnp.zeros((INNER,), dtype=jnp.float32)
        A = jax.random.normal(ks[3], (G, D), dtype=jnp.float32)
        Q, _ = jnp.linalg.qr(A.T)
        W_slice = Q[:, :G].astype(jnp.float32)
        b_slice = jnp.zeros((G,), dtype=jnp.float32)
        W_q = jax.random.normal(ks[4], (D, D), dtype=jnp.float32) * s(D)
        W_k = jax.random.normal(ks[5], (D, D), dtype=jnp.float32) * s(D)
        W_v = jax.random.normal(ks[6], (D, D), dtype=jnp.float32) * s(D)
        W_out = jax.random.normal(ks[7], (INNER, DIM), dtype=jnp.float32) * s(INNER)
        b_out = jnp.zeros((DIM,), dtype=jnp.float32)
        temperature = jnp.ones((1, H, 1, 1), dtype=jnp.float32) * 0.5
        return {'x': x, 'W_fx': W_fx, 'b_fx': b_fx, 'W_x': W_x, 'b_x': b_x, 'W_slice': W_slice, 'b_slice': b_slice, 'W_q': W_q, 'W_k': W_k, 'W_v': W_v, 'W_out': W_out, 'b_out': b_out, 'temperature': temperature}
    _L0_ffn_all = _L0_ffn_setup()
    _L0_ffn_in = {k: v for k, v in _L0_ffn_all.items() if k in ('W_fx', 'b_fx', 'W_x', 'b_x', 'W_slice', 'b_slice', 'W_q', 'W_k', 'W_v', 'W_out', 'b_out', 'temperature')}
    del _L0_ffn_all

    def _L1_gnn_setup():
        import jax, jax.numpy as jnp
        import numpy as np
        N_NODES = 6250
        N_EDGES = 100000
        D_IN = 256
        D_OUT = 256
        N_REL = 8
        key = jax.random.key(seed)
        k_x, k_ei, k_et, k_w = jax.random.split(key, 4)
        x = jax.random.normal(k_x, (N_NODES, D_IN), dtype=jnp.float32)
        edge_index = jax.random.randint(k_ei, (2, N_EDGES), 0, N_NODES, dtype=jnp.int32)
        edge_type = jax.random.randint(k_et, (N_EDGES,), 0, N_REL, dtype=jnp.int32)
        limit = float(np.sqrt(6.0 / (D_IN + D_OUT)))
        weight = jax.random.uniform(k_w, (N_REL, D_IN, D_OUT), dtype=jnp.float32, minval=-limit, maxval=limit)
        bias = jnp.zeros((D_OUT,), dtype=jnp.float32)
        return {'x': x, 'edge_index': edge_index, 'edge_type': edge_type, 'weight': weight, 'bias': bias}
    _L1_gnn_all = _L1_gnn_setup()
    _L1_gnn_in = {k: v for k, v in _L1_gnn_all.items() if k in ('weight', 'bias')}
    del _L1_gnn_all

    def _L1_mix_setup():
        import jax, jax.numpy as jnp
        import numpy as np
        A, Bc, Cc = (0.5, 1.0, 1.0)
        H = 8
        EPS = 1e-12

        def _normalize(t):
            n = jnp.linalg.norm(t, axis=-1, keepdims=True)
            return t / jnp.maximum(n, EPS)
        key = jax.random.key(seed)
        ks = jax.random.split(key, 5)
        B, N, C = (8, 256, 256)
        D = C // H
        x = jax.random.normal(ks[0], (B, N, C), dtype=jnp.float32)
        Wqkv = jax.random.normal(ks[1], (3 * H * D, C), dtype=jnp.float32) * 0.02
        bqkv = jnp.zeros((3 * H * D,), dtype=jnp.float32)
        Wproj = jax.random.normal(ks[2], (C, H * D), dtype=jnp.float32) * 0.02
        bproj = jnp.zeros((C,), dtype=jnp.float32)
        temperature = jnp.ones((1, H, 1, 1), dtype=jnp.float32)
        return {'x': x, 'Wqkv': Wqkv, 'bqkv': bqkv, 'Wproj': Wproj, 'bproj': bproj, 'temperature': temperature}
    _L1_mix_all = _L1_mix_setup()
    _L1_mix_in = {k: v for k, v in _L1_mix_all.items() if k in ('Wqkv', 'bqkv', 'Wproj', 'bproj', 'temperature')}
    del _L1_mix_all

    def _L1_ffn_setup():
        import jax, jax.numpy as jnp
        import numpy as np
        B, T, D, H, E = (16, 512, 256, 512, 8)
        key = jax.random.key(seed)
        ks = jax.random.split(key, 5)
        x = jax.random.normal(ks[0], (B, T, D), dtype=jnp.float32)
        gate_w = jax.random.normal(ks[1], (D, E), dtype=jnp.float32) * 0.02
        gate_b = jnp.zeros((E,), dtype=jnp.float32)
        W1 = jax.random.normal(ks[2], (E, D, H), dtype=jnp.float32) * 0.02
        b1 = jnp.zeros((E, H), dtype=jnp.float32)
        W2 = jax.random.normal(ks[3], (E, H, D), dtype=jnp.float32) * 0.02
        b2 = jnp.zeros((E, D), dtype=jnp.float32)
        return {'x': x, 'gate_w': gate_w, 'gate_b': gate_b, 'W1': W1, 'b1': b1, 'W2': W2, 'b2': b2}
    _L1_ffn_all = _L1_ffn_setup()
    _L1_ffn_in = {k: v for k, v in _L1_ffn_all.items() if k in ('gate_w', 'gate_b', 'W1', 'b1', 'W2', 'b2')}
    del _L1_ffn_all
    return {'x': x, 'src': src, 'dst': dst, 'edge_type_8': edge_type_8, 'L0_gnn_Wp': _L0_gnn_in['Wp'], 'L0_gnn_a_src': _L0_gnn_in['a_src'], 'L0_gnn_a_trg': _L0_gnn_in['a_trg'], 'L0_gnn_Wskip': _L0_gnn_in['Wskip'], 'L0_gnn_bias': _L0_gnn_in['bias'], 'L0_mix_Wq': _L0_mix_in['Wq'], 'L0_mix_Wk': _L0_mix_in['Wk'], 'L0_mix_Wv': _L0_mix_in['Wv'], 'L0_mix_Wm': _L0_mix_in['Wm'], 'L0_mix_W1': _L0_mix_in['W1'], 'L0_mix_W2': _L0_mix_in['W2'], 'L0_mix_g1': _L0_mix_in['g1'], 'L0_mix_b1': _L0_mix_in['b1'], 'L0_mix_g2': _L0_mix_in['g2'], 'L0_mix_b2': _L0_mix_in['b2'], 'L0_ffn_W_fx': _L0_ffn_in['W_fx'], 'L0_ffn_b_fx': _L0_ffn_in['b_fx'], 'L0_ffn_W_x': _L0_ffn_in['W_x'], 'L0_ffn_b_x': _L0_ffn_in['b_x'], 'L0_ffn_W_slice': _L0_ffn_in['W_slice'], 'L0_ffn_b_slice': _L0_ffn_in['b_slice'], 'L0_ffn_W_q': _L0_ffn_in['W_q'], 'L0_ffn_W_k': _L0_ffn_in['W_k'], 'L0_ffn_W_v': _L0_ffn_in['W_v'], 'L0_ffn_W_out': _L0_ffn_in['W_out'], 'L0_ffn_b_out': _L0_ffn_in['b_out'], 'L0_ffn_temperature': _L0_ffn_in['temperature'], 'L1_gnn_weight': _L1_gnn_in['weight'], 'L1_gnn_bias': _L1_gnn_in['bias'], 'L1_mix_Wqkv': _L1_mix_in['Wqkv'], 'L1_mix_bqkv': _L1_mix_in['bqkv'], 'L1_mix_Wproj': _L1_mix_in['Wproj'], 'L1_mix_bproj': _L1_mix_in['bproj'], 'L1_mix_temperature': _L1_mix_in['temperature'], 'L1_ffn_gate_w': _L1_ffn_in['gate_w'], 'L1_ffn_gate_b': _L1_ffn_in['gate_b'], 'L1_ffn_W1': _L1_ffn_in['W1'], 'L1_ffn_b1': _L1_ffn_in['b1'], 'L1_ffn_W2': _L1_ffn_in['W2'], 'L1_ffn_b2': _L1_ffn_in['b2']}

def reference(x, src, dst, edge_type_8, L0_gnn_Wp, L0_gnn_a_src, L0_gnn_a_trg, L0_gnn_Wskip, L0_gnn_bias, L0_mix_Wq, L0_mix_Wk, L0_mix_Wv, L0_mix_Wm, L0_mix_W1, L0_mix_W2, L0_mix_g1, L0_mix_b1, L0_mix_g2, L0_mix_b2, L0_ffn_W_fx, L0_ffn_b_fx, L0_ffn_W_x, L0_ffn_b_x, L0_ffn_W_slice, L0_ffn_b_slice, L0_ffn_W_q, L0_ffn_W_k, L0_ffn_W_v, L0_ffn_W_out, L0_ffn_b_out, L0_ffn_temperature, L1_gnn_weight, L1_gnn_bias, L1_mix_Wqkv, L1_mix_bqkv, L1_mix_Wproj, L1_mix_bproj, L1_mix_temperature, L1_ffn_gate_w, L1_ffn_gate_b, L1_ffn_W1, L1_ffn_b1, L1_ffn_W2, L1_ffn_b2):
    import jax
    import jax.numpy as jnp

    def _L0_gnn_ref(node_features, edge_index, Wp, a_src, a_trg, Wskip, bias):
        import jax, jax.numpy as jnp
        import numpy as np
        N, E, FIN, H, FO = (6250, 100000, 256, 8, 32)
        x = node_features
        src, trg = (edge_index[0], edge_index[1])
        proj = (x @ Wp.T).reshape(-1, H, FO)
        scores_src = jnp.sum(proj * a_src, axis=-1)
        scores_trg = jnp.sum(proj * a_trg, axis=-1)
        s = scores_src[src] + scores_trg[trg]
        s = jax.nn.leaky_relu(s, negative_slope=0.2)
        s = s - jnp.max(s)
        exp_s = jnp.exp(s)
        denom = jax.ops.segment_sum(exp_s, trg, num_segments=N)
        attn = exp_s / (denom[trg] + 1e-16)
        weighted = proj[src] * attn[:, :, None]
        out = jax.ops.segment_sum(weighted, trg, num_segments=N)
        out = out + (x @ Wskip.T).reshape(-1, H, FO)
        out = out.reshape(-1, H * FO) + bias
        return jax.nn.elu(out)

    def _L0_mix_ref(x, Wq, Wk, Wv, Wm, W1, W2, g1, b1, g2, b2):
        import jax, jax.numpy as jnp
        import numpy as np
        NHEAD = 8
        ATT_EPS = 1e-06
        LN_EPS = 1e-05

        def _layernorm(x, g, b):
            mu = jnp.mean(x, axis=-1, keepdims=True)
            var = jnp.mean(jnp.square(x - mu), axis=-1, keepdims=True)
            return (x - mu) * jax.lax.rsqrt(var + LN_EPS) * g + b
        N, L, C = x.shape
        H = NHEAD
        D = C // H
        q = (x @ Wq).reshape(N, L, H, D)
        k = (x @ Wk).reshape(N, L, H, D)
        v = (x @ Wv).reshape(N, L, H, D)
        Q = jax.nn.elu(q) + 1.0
        K = jax.nn.elu(k) + 1.0
        v = v / L
        KV = jnp.einsum('nshd,nshv->nhdv', K, v)
        Z = 1.0 / (jnp.einsum('nlhd,nhd->nlh', Q, K.sum(axis=1)) + ATT_EPS)
        msg = jnp.einsum('nlhd,nhdv,nlh->nlhv', Q, KV, Z) * L
        msg = msg.reshape(N, L, C) @ Wm
        msg = _layernorm(msg, g1, b1)
        h = jnp.concatenate([x, msg], axis=-1) @ W1
        h = jax.nn.relu(h) @ W2
        msg = _layernorm(h, g2, b2)
        return x + msg

    def _L0_ffn_ref(x, W_fx, b_fx, W_x, b_x, W_slice, b_slice, W_q, W_k, W_v, W_out, b_out, temperature):
        import jax, jax.numpy as jnp
        import numpy as np
        DIM = 256
        H = 8
        D = 64
        G = 64
        INNER = H * D
        SCALE = D ** (-0.5)
        B, N, _ = x.shape
        fx_mid = (x @ W_fx + b_fx).reshape(B, N, H, D).transpose(0, 2, 1, 3)
        x_mid = (x @ W_x + b_x).reshape(B, N, H, D).transpose(0, 2, 1, 3)
        temp = jnp.clip(temperature, 0.1, 5.0)
        slice_weights = jax.nn.softmax((x_mid @ W_slice + b_slice) / temp, axis=-1)
        slice_norm = slice_weights.sum(axis=2)
        slice_token = jnp.einsum('bhnc,bhng->bhgc', fx_mid, slice_weights)
        slice_token = slice_token / (slice_norm[..., None] + 1e-05)
        q = slice_token @ W_q
        k = slice_token @ W_k
        v = slice_token @ W_v
        attn = jax.nn.softmax(jnp.einsum('bhgc,bhkc->bhgk', q, k) * SCALE, axis=-1)
        out_slice = jnp.einsum('bhgk,bhkc->bhgc', attn, v)
        out_x = jnp.einsum('bhgc,bhng->bhnc', out_slice, slice_weights)
        out_x = out_x.transpose(0, 2, 1, 3).reshape(B, N, INNER)
        return out_x @ W_out + b_out

    def _L1_gnn_ref(x, edge_index, edge_type, weight, bias):
        import jax, jax.numpy as jnp
        import numpy as np
        N_NODES = 6250
        N_EDGES = 100000
        D_IN = 256
        D_OUT = 256
        N_REL = 8
        num_nodes = x.shape[0]
        row, col = (edge_index[0], edge_index[1])
        xt = jnp.einsum('ni,rio->rno', x, weight)
        messages = xt[edge_type, col]
        out = jax.ops.segment_sum(messages, row, num_segments=num_nodes)
        return jax.nn.relu(out + bias)

    def _L1_mix_ref(x, Wqkv, bqkv, Wproj, bproj, temperature):
        import jax, jax.numpy as jnp
        import numpy as np
        A, Bc, Cc = (0.5, 1.0, 1.0)
        H = 8
        EPS = 1e-12

        def _normalize(t):
            n = jnp.linalg.norm(t, axis=-1, keepdims=True)
            return t / jnp.maximum(n, EPS)
        B, N, C = x.shape
        D = C // H
        scale = float(D) ** 0.25
        qkv = (x @ Wqkv.T + bqkv).reshape(B, N, 3, H, D)
        qkv = jnp.transpose(qkv, (2, 0, 3, 1, 4))
        q, k, v = (qkv[0], qkv[1], qkv[2])
        q = q * scale
        v1 = jnp.concatenate([jnp.ones((B, H, N, 1), dtype=v.dtype), v], axis=-1)
        qn = _normalize(q) * (scale * temperature)
        kn = _normalize(k) * scale
        vN = v1 / N
        kv_mod = jnp.einsum('bhni,bhnj,bhne->bhije', kn, kn, vN)
        kv = jnp.einsum('bhnd,bhne->bhde', kn, vN)
        vsum = jnp.sum(vN, axis=-2)[:, :, None, :]
        y = A * jnp.einsum('bhni,bhnj,bhije->bhne', qn, qn, kv_mod) + scale ** 2 * Bc * jnp.einsum('bhnd,bhde->bhne', qn, kv) + scale ** 4 * Cc * vsum
        y_norm, y = (y[..., :1], y[..., 1:])
        y = y / y_norm
        out = jnp.transpose(y, (0, 2, 1, 3)).reshape(B, N, H * D)
        return out @ Wproj.T + bproj

    def _L1_ffn_ref(x, gate_w, gate_b, W1, b1, W2, b2):
        import jax, jax.numpy as jnp
        import numpy as np
        B, T, D, H, E = (16, 512, 256, 512, 8)
        Bb, Tt, Dd = x.shape
        Ee = gate_w.shape[1]
        xf = x.reshape(-1, Dd)
        N = xf.shape[0]
        logits = xf @ gate_w + gate_b
        probs = jax.nn.softmax(logits, axis=-1)
        top2_vals, top2_idx = jax.lax.top_k(probs, 2)
        cw = jnp.zeros((N, Ee), dtype=xf.dtype).at[jnp.arange(N)[:, None], top2_idx].add(top2_vals)

        def step(acc, params):
            w1, bb1, w2, bb2, we = params
            h = jax.nn.gelu(xf @ w1 + bb1, approximate=False)
            y = h @ w2 + bb2
            return (acc + we[:, None] * y, None)
        out, _ = jax.lax.scan(step, jnp.zeros_like(xf), (W1, b1, W2, b2, cw.T))
        return out.reshape(Bb, Tt, Dd)
    edge_index = jnp.stack([src, dst])
    xn = _layernorm(x, axis=-1)
    x = x + _L0_gnn_ref(xn, edge_index, L0_gnn_Wp, L0_gnn_a_src, L0_gnn_a_trg, L0_gnn_Wskip, L0_gnn_bias) + _L0_mix_ref(xn[None], L0_mix_Wq, L0_mix_Wk, L0_mix_Wv, L0_mix_Wm, L0_mix_W1, L0_mix_W2, L0_mix_g1, L0_mix_b1, L0_mix_g2, L0_mix_b2)[0]
    x = x + _L0_ffn_ref(_layernorm(x, axis=-1)[None], L0_ffn_W_fx, L0_ffn_b_fx, L0_ffn_W_x, L0_ffn_b_x, L0_ffn_W_slice, L0_ffn_b_slice, L0_ffn_W_q, L0_ffn_W_k, L0_ffn_W_v, L0_ffn_W_out, L0_ffn_b_out, L0_ffn_temperature)[0]
    xn = _layernorm(x, axis=-1)
    x = x + _L1_gnn_ref(xn, edge_index, edge_type_8, L1_gnn_weight, L1_gnn_bias) + _L1_mix_ref(xn[None], L1_mix_Wqkv, L1_mix_bqkv, L1_mix_Wproj, L1_mix_bproj, L1_mix_temperature)[0]
    x = x + _L1_ffn_ref(_layernorm(x, axis=-1)[None], L1_ffn_gate_w, L1_ffn_gate_b, L1_ffn_W1, L1_ffn_b1, L1_ffn_W2, L1_ffn_b2)[0]
    return x

_drawn_inputs = setup_inputs


def setup_inputs(seed=0):
    import zlib

    import numpy as np

    out = dict(_drawn_inputs(seed))
    spreads = {'L0_gnn_bias': (0.0, 0.1),
     'L0_mix_g1': (1.0, 0.2),
     'L0_mix_b1': (0.0, 0.1),
     'L0_mix_g2': (1.0, 0.2),
     'L0_mix_b2': (0.0, 0.1),
     'L0_ffn_b_fx': (0.0, 0.1),
     'L0_ffn_b_x': (0.0, 0.8),
     'L0_ffn_b_slice': (0.0, 0.8),
     'L0_ffn_b_out': (0.0, 0.1),
     'L0_ffn_temperature': (0.5, 0.6),
     'L1_gnn_bias': (0.0, 0.629),
     'L1_mix_bqkv': (0.0, 0.8),
     'L1_mix_bproj': (0.0, 0.446),
     'L1_mix_temperature': (1.0, 0.6),
     'L1_ffn_gate_b': (0.0, 0.8),
     'L1_ffn_b1': (0.0, 0.8),
     'L1_ffn_b2': (0.0, 0.8)}
    factors = {'L0_gnn_a_trg': 5.905,
     'L0_ffn_W_x': 8.0,
     'L0_ffn_W_slice': 8.0,
     'L0_ffn_W_q': 8.0,
     'L0_ffn_W_k': 8.0,
     'L1_mix_Wqkv': 8.0,
     'L1_mix_Wproj': 5.851,
     'L1_ffn_gate_w': 8.0,
     'L1_ffn_W1': 8.0,
     'L1_ffn_W2': 8.0}
    for name, (base, spread) in spreads.items():
        noise = np.random.default_rng([zlib.crc32(name.encode()), seed]).standard_normal(out[name].shape)
        drawn = base * np.exp(spread * noise) if base else spread * noise
        out[name] = jnp.asarray(drawn.astype(out[name].dtype))
    for name, factor in factors.items():
        out[name] = (out[name] * factor).astype(out[name].dtype)
    return out
```

```python
from contextlib import ExitStack

import concourse.bass as bass
from concourse import mybir

ALU = mybir.AluOpType
ACT = mybir.ActivationFunctionType
AX = mybir.AxisListType
F32 = mybir.dt.float32
BF16 = mybir.dt.bfloat16
I32 = mybir.dt.int32
I16 = mybir.dt.int16
RMAX = bass.bass_isa.ReduceOp.max

N, C, E = 6250, 256, 200000
P = 125
NT = N // P
H, D = 8, 32
EC = E // P
LANES = 128
CH = (E + NT * (LANES - 1)) // LANES
G = 13
NG = CH // G
assert NG * G == CH and NT * P == N and EC * P == E
NOBODY = 127
TW = C + H
LN_EPS = 1e-5
NEG = -1e30
R = 8
SL = 64
DS = 64


class Shared:
    pass


def in_units(eng, body, n, w=2):
    for u in range(w):
        body(u, u)
    with eng.Fori(1, n // w) as i:
        for u in range(w):
            body(i * w + u, u)
    for u in range(n % w):
        body(n - n % w + u, u)


def in_units_last(eng, body):
    for n in range(2):
        body(n, n, False)
    with eng.Fori(1, NT // 2 - 1) as i:
        for u in range(2):
            body(i * 2 + u, u, False)
    for n in range(NT - 2, NT):
        body(n, n % 2, n == NT - 1)


def first(unit):
    return isinstance(unit, int) and unit == 0


def later(unit, w=2):
    return not (isinstance(unit, int) and unit < w)


def constants(nc, m):
    sb = m.sb
    m.ident = sb("ident", [128, 128], F32)
    m.ones = sb("ones", [128, 128], F32)
    m.count_p = sb("count_p", [128, P], F32)
    m.count_t = sb("count_t", [P, NT], F32)
    m.below = sb("below", [P, P], F32)
    m.s_const = m.sem("s_const")
    with m.block() as block:
        @block.gpsimd
        def _(pool):
            pool.memset(m.ident[:, :], 0.0).then_inc(m.s_const, 1)
            pool.memset(m.ones[:, :], 1.0).then_inc(m.s_const, 1)
            pool.iota(m.count_p[:, :], [[1, P]], base=0, channel_multiplier=0,
                      allow_small_or_imprecise_dtypes=True)
            pool.iota(m.count_t[:, :], [[1, NT]], base=0, channel_multiplier=0,
                      allow_small_or_imprecise_dtypes=True)
            pool.wait_ge(m.s_const, 2)
            pool.affine_select(out=m.ident[:, :], in_=m.ident[:, :], compare_op=ALU.not_equal, fill=1.0,
                               base=0, pattern=[[-1, 128]], channel_multiplier=1)
            pool.affine_select(out=m.below[:, :], in_=m.ones[0:P, 0:P], compare_op=ALU.is_gt, fill=0.0,
                               base=0, pattern=[[1, P]], channel_multiplier=-1)


def row_statistics(nc, m, rows, mean, rstd, tmp, name):
    six = tmp[:, 0:NT * 6].rearrange("p (t s) -> p t s", s=6)
    d = tmp[:, NT * 6:NT * 7]
    v = tmp[:, NT * 7:NT * 8]
    s_var, s_std = m.sem(f"s_var_{name}"), m.sem(f"s_std_{name}")
    with m.block() as block:
        @block.vector
        def _(dve):
            with dve.Fori(0, NT // 5) as i:
                for u in range(5):
                    dve.bn_stats(six[:, i * 5 + u, :], rows[:, i * 5 + u, :])
            dve.drain()
            dve.tensor_tensor(mean[:, :], six[:, :, 1], six[:, :, 4], ALU.add)
            dve.tensor_tensor(d, six[:, :, 1], six[:, :, 4], ALU.subtract)
            dve.tensor_tensor(v, six[:, :, 2], six[:, :, 5], ALU.add)
            dve.drain()
            dve.tensor_scalar(mean[:, :], mean[:, :], 0.5, None, ALU.mult)
            dve.scalar_tensor_tensor(out=d, in0=d, scalar=0.25, in1=d, op0=ALU.mult, op1=ALU.mult)
            dve.tensor_scalar(v, v, 1.0 / C, LN_EPS, ALU.mult, ALU.add)
            dve.drain()
            dve.tensor_tensor(v, v, d, ALU.add).then_inc(s_var, 1)
            dve.wait_ge(s_std, 1)
            dve.reciprocal(rstd[:, :], v)

        @block.scalar
        def _(act):
            act.wait_ge(s_var, 1)
            act.activation(v, v, ACT.Sqrt).then_inc(s_std, 1)


def load_inputs(nc, m, a):
    m.x = m.sb("x", [P, NT, C], F32)
    m.s_x = m.sem("s_x")
    with m.block() as block:
        @block.sync
        def _(sp):
            sp.dma_start(m.x[:, :, :], a["x"].rearrange("(t p) c -> p t c", p=P)).then_inc(m.s_x, 16)
            sp.wait_ge(m.s_x, 16)


def project_l0(nc, m, a):
    with ExitStack() as ctx:
        sb, ps, sem = m.scope(nc, ctx)
        w_ps = sb("w_ps", [128, 2, 2 * C], F32)
        w_kv = sb("w_kv", [128, 2, 2 * C], F32)
        w_sc = sb("w_sc", [128, 2, 2 * H], F32)
        a_row = sb("a_row", [128, 2, C], F32)
        prod = sb("prod", [128, 2, 2, C], F32)
        xn = [sb(f"xn{u}", [P, C], F32) for u in range(2)]
        xt = [sb(f"xt{u}", [128, 2, P], F32) for u in range(2)]
        row = [sb(f"row{u}", [P, TW], F32) for u in range(2)]
        skip = [sb(f"skip{u}", [P, C], F32) for u in range(2)]
        kmin = [sb(f"kmin{u}", [P, C], F32) for u in range(2)]
        kf = [sb(f"kf{u}", [P, C], F32) for u in range(2)]
        vf = [sb(f"vf{u}", [P, 2, 129], F32) for u in range(2)]
        pad_row = sb("pad_row", [1, TW], F32)
        zero = sb("zero", [128, 258], F32)
        p_t = [ps(f"p_t{u}", [128, 512]) for u in range(2)]
        p_a = [ps(f"p_a{u}", [128, 512]) for u in range(2)]
        p_b = [ps(f"p_b{u}", [128, 512]) for u in range(2)]
        p_s = ps("p_s", [128, 512])
        p_kv = ps("p_kv", [128, 512])
        s_w, s_wsc, s_zero, s_pad = sem("s_w"), sem("s_wsc"), sem("s_zero"), sem("s_pad")
        s_xn, s_tr, s_xt, s_mm, s_act, s_dve = (sem(x) for x in (
            "s_xn", "s_tr", "s_xt", "s_mm", "s_act", "s_dve"))
        s_kmin, s_kexp, s_kv, s_mkv = sem("s_kmin"), sem("s_kexp"), sem("s_kv"), sem("s_mkv")
        s_sc = sem("s_sc")
        s_out = [sem(f"s_out{u}") for u in range(2)]
        with m.block() as block:
            @block.sync
            def _(sp):
                sp.dma_start(w_ps[:, :, 0:C], a["L0_gnn_Wp"].rearrange("(c p) n -> p c n", p=128)).then_inc(s_w, 16)
                sp.dma_start(w_ps[:, :, C:2 * C], a["L0_gnn_Wskip"].rearrange("(c p) n -> p c n", p=128)).then_inc(s_w, 16)
                sp.dma_start(w_kv[:, :, 0:C], a["L0_mix_Wk"].rearrange("(c p) n -> p c n", p=128)).then_inc(s_w, 16)
                sp.dma_start(w_kv[:, :, C:2 * C], a["L0_mix_Wv"].rearrange("(c p) n -> p c n", p=128)).then_inc(s_w, 16)
                sp.dma_start(a_row[:, 0, :], a["L0_gnn_a_src"].rearrange("a h f -> a (h f)").broadcast_to((128, C))).then_inc(s_w, 16)
                sp.dma_start(a_row[:, 1, :], a["L0_gnn_a_trg"].rearrange("a h f -> a (h f)").broadcast_to((128, C))).then_inc(s_w, 16)
                sp.wait_ge(s_zero, 3)
                sp.dma_start(m.table0[N:N + 1, :], pad_row[:, :]).then_inc(s_pad, 16)

                def store(n, u):
                    sp.wait_ge(s_act, n + 1)
                    sp.wait_ge(s_sc, n + 1)
                    sp.dma_start(m.table0[bass.ds(n * P, P), :], row[u][:, :]).then_inc(s_out[u], 16)
                    sp.dma_start(m.skip_rows[bass.ds(n * P, P), :], skip[u][:, :]).then_inc(s_out[u], 16)

                in_units(sp, store, NT)
                sp.wait_ge(s_out[0], 16 * NT)
                sp.wait_ge(s_out[1], 16 * NT)
                sp.wait_ge(s_pad, 16)

            @block.scalar
            def _(act):
                def step(n, u):
                    if later(n):
                        act.wait_ge(s_tr, n - 1)
                    act.activation(xn[u][:, :], m.x[:, n, :], ACT.Identity, scale=m.rstd[:, bass.ds(n, 1)],
                                   bias=m.nmr[:, bass.ds(n, 1)]).then_inc(s_xn, 1)
                    act.wait_ge(s_tr, n + 1)
                    if later(n):
                        act.wait_ge(s_mm, n - 1)
                    act.copy(xt[u][:, :, :], p_t[u][:, 0:2 * P].rearrange("p (c n) -> p c n", c=2)).then_inc(s_xt, 1)
                    act.wait_ge(s_kmin, n + 1)
                    if later(n):
                        act.wait_ge(s_kv, n - 1)
                    act.activation(kf[u][:, :], kmin[u][:, :], ACT.Exp).then_inc(s_kexp, 1)
                    if later(n):
                        act.wait_ge(s_out[u], (n // 2) * 32 if isinstance(n, int) else (n - u) * 16)
                    act.copy(row[u][:, 0:C], p_a[u][0:P, 0:C])
                    act.copy(skip[u][:, :], p_a[u][0:P, C:2 * C]).then_inc(s_act, 1)

                in_units(act, step, NT)

            @block.vector
            def _(dve):
                dve.memset(pad_row[:, 0:C], 0.0).then_inc(s_zero, 1)
                dve.memset(pad_row[:, C:TW], NEG).then_inc(s_zero, 1)
                dve.memset(zero[:, :], 0.0).then_inc(s_zero, 1)
                for u in range(2):
                    dve.memset(vf[u][:, :, 128:129], 1.0)
                dve.wait_ge(s_w, 16 * 6)
                for c in range(2):
                    for k in range(2):
                        dve.tensor_tensor(prod[:, c, k, :], w_ps[:, c, 0:C], a_row[:, k, :], ALU.mult)
                dve.drain()
                for c in range(2):
                    dve.tensor_reduce(w_sc[:, c, :], prod[:, c, :, :].rearrange("p k (h f) -> p (k h) f", f=D),
                                      AX.X, ALU.add).then_inc(s_wsc, 1)

                def step(n, u):
                    dve.wait_ge(s_mm, n + 1)
                    if later(n):
                        dve.wait_ge(s_kexp, n - 1)
                        dve.wait_ge(s_mkv, n - 1)
                        dve.wait_ge(s_out[u], (n // 2) * 32 if isinstance(n, int) else (n - u) * 16)
                    dve.tensor_scalar(kmin[u][:, :], p_b[u][0:P, 0:C], 0.0, None, ALU.min).then_inc(s_kmin, 1)
                    dve.tensor_copy(vf[u][:, :, 0:128],
                                    p_b[u][0:P, C:2 * C].rearrange("p (g v) -> p g v", g=2))
                    dve.tensor_copy(row[u][:, C:TW], p_s[0:P, 0:H])
                    dve.tensor_copy(m.score[:, n, :], p_s[0:P, 0:2 * H]).then_inc(s_sc, 1)
                    dve.wait_ge(s_kexp, n + 1)
                    dve.scalar_tensor_tensor(out=kf[u][:, :], in0=p_b[u][0:P, 0:C], scalar=0.0, in1=kf[u][:, :],
                                             op0=ALU.max, op1=ALU.add).then_inc(s_kv, 1)

                in_units(dve, step, NT)
                dve.wait_ge(s_mkv, NT)
                dve.tensor_copy(m.kv_sum[:, :], p_kv[:, 0:258])

            @block.tensor
            def _(pe):
                pe.wait_ge(s_zero, 3)
                pe.matmul(p_kv[:, 0:258], zero[:, 0:128], zero[:, :], start=True, stop=False, skip_group_check=True)

                def fold(n, u):
                    pe.wait_ge(s_kv, n + 1)
                    for g in range(2):
                        mm = pe.matmul(p_kv[:, 129 * g:129 * g + 129], kf[u][:, 128 * g:128 * g + 128],
                                       vf[u][:, g, :], start=False, stop=False, skip_group_check=True)
                    mm.then_inc(s_mkv, 1)

                def step(n, u):
                    pe.wait_ge(s_xn, n + 1)
                    if later(n):
                        pe.wait_ge(s_xt, n - 1)
                    for c in range(2):
                        mm = pe.transpose(p_t[u][:, c * P:c * P + P], xn[u][:, c * 128:c * 128 + 128],
                                          m.ident[0:P, 0:P])
                    mm.then_inc(s_tr, 1)
                    if not (isinstance(n, int) and n == 0):
                        fold(n - 1, 1 - u)
                    pe.wait_ge(s_xt, n + 1)
                    if isinstance(n, int) and n == 0:
                        pe.wait_ge(s_wsc, 2)
                    if later(n):
                        pe.wait_ge(s_act, n - 1)
                        pe.wait_ge(s_kv, n - 1)
                    for c in range(2):
                        pe.matmul(p_a[u][0:P, :], xt[u][:, c, :], w_ps[:, c, :], start=c == 0, stop=c == 1)
                    for c in range(2):
                        pe.matmul(p_b[u][0:P, :], xt[u][:, c, :], w_kv[:, c, :], start=c == 0, stop=c == 1)
                    if not (isinstance(n, int) and n == 0):
                        pe.wait_ge(s_sc, n)
                    for c in range(2):
                        mm = pe.matmul(p_s[0:P, 0:2 * H], xt[u][:, c, :], w_sc[:, c, :], start=c == 0, stop=c == 1)
                    mm.then_inc(s_mm, 1)

                in_units(pe, step, NT)
                fold(NT - 1, 1)



def rank_edges(nc, m, key, row_of, pi, tile_of, name):
    with ExitStack() as ctx:
        sb, ps, sem = m.scope(nc, ctx)
        key_i = sb(f"key_i_{name}", [P, EC], I32)
        row_i = [sb(f"row_i{k}_{name}", [P, EC], I32) for k in range(len(row_of))]
        key_f = sb(f"key_f_{name}", [P, EC], F32)
        tile_i = sb(f"tile_i_{name}", [P, EC], I32)
        tile16 = sb(f"tile16_{name}", [P, EC], BF16)
        within = sb(f"within_{name}", [P, EC], F32)
        row_f = sb(f"row_f_{name}", [P, EC], F32)
        mask = sb(f"mask_{name}", [P, EC], BF16)
        one16 = sb(f"one16_{name}", [P, EC], BF16)
        count = sb(f"count_{name}", [P, NT], F32)
        offset = sb(f"offset_{name}", [P, NT], F32)
        n_i = sb(f"n_i_{name}", [NT, 1], I32)
        n_col = sb(f"n_col_{name}", [NT, 1], F32)
        n_wide = sb(f"n_wide_{name}", [NT, P], F32)
        end = sb(f"end_{name}", [NT, 1], F32)
        upto = sb(f"upto_{name}", [NT, NT], F32)
        chunk_no = sb(f"chunk_no_{name}", [NT, CH], F32)
        p_pre, p_tot, p_start, p_end, = (ps(f"{x}_{name}", [128, 512]) for x in ("p_pre", "p_tot", "p_start", "p_end"))
        p_tile = [ps(f"p_tile{k}_{name}", [128, 512]) for k in range(4)]
        s_load, s_iota, s_count, s_tot, s_n, s_sum, s_over, s_tile = (sem(f"{x}_{name}") for x in (
            "s_load", "s_iota", "s_count", "s_tot", "s_n", "s_sum", "s_over", "s_tile"))
        slot_f, running = key_f, row_f
        with m.block() as block:
            @block.sync
            def _(sp):
                sp.dma_start(key_i[:, :], key.rearrange("(p j) -> p j", p=P)).then_inc(s_load, 16)
                for k, r in enumerate(row_of):
                    sp.dma_start(row_i[k][:, :], r.rearrange("(p j) -> p j", p=P)).then_inc(s_load, 16)

            @block.vector
            def _(dve):
                dve.memset(one16[:, :], 1.0)
                dve.tensor_tensor(upto[:, :], m.below[0:NT, 0:NT], m.ident[0:NT, 0:NT], ALU.add)
                dve.wait_ge(s_load, 16 * (1 + len(row_of)))
                dve.tensor_copy(key_f[:, :], key_i[:, :])
                dve.drain()
                dve.tensor_scalar(tile_i[:, :], key_f[:, :], -float(P // 2), 1.0 / P, ALU.add, ALU.mult)
                dve.drain()
                dve.tensor_copy(tile16[:, :], tile_i[:, :])
                dve.scalar_tensor_tensor(out=within[:, :], in0=tile_i[:, :], scalar=-float(P), in1=key_f[:, :],
                                         op0=ALU.mult, op1=ALU.add)
                if len(row_of) == 2:
                    dve.scalar_tensor_tensor(out=row_f[:, :], in0=row_i[0][:, :], scalar=float(N), in1=row_i[1][:, :],
                                             op0=ALU.mult, op1=ALU.add)
                else:
                    dve.tensor_copy(row_f[:, :], row_i[0][:, :])
                dve.drain()
                dve.scalar_tensor_tensor(out=pi[:, :, 1], in0=row_f[:, :], scalar=float(LANES), in1=within[:, :],
                                         op0=ALU.mult, op1=ALU.add)
                with dve.Fori(0, NT) as b:
                    dve.tensor_scalar(mask[:, :], tile16[:, :], m.count_t[:, bass.ds(b, 1)], 0.0, ALU.is_equal,
                                      ALU.add, accum_out=count[:, bass.ds(b, 1)])
                    dve.drain()
                dve.drain().then_inc(s_count, 1)
                dve.wait_ge(s_tot, 1)
                dve.tensor_scalar(n_i[:, :], p_tot[0:NT, 0:1], float(LANES - 1), None, ALU.add)
                dve.drain()
                dve.tensor_scalar(n_i[:, :], n_i[:, :], 7, None, ALU.arith_shift_right)
                dve.drain()
                dve.tensor_copy(n_col[:, :], n_i[:, :])
                dve.drain()
                dve.tensor_scalar(n_wide[:, :], m.ones[0:NT, 0:P], n_col[:, 0:1], None, ALU.mult).then_inc(s_n, 1)
                dve.wait_ge(s_sum, 1)
                dve.tensor_copy(end[:, :], p_end[0:NT, 0:1])
                dve.tensor_scalar(offset[:, :], p_start[0:P, 0:NT], float(LANES), -1.0, ALU.mult, ALU.add)
                dve.wait_ge(s_iota, 1)
                dve.drain()
                dve.tensor_tensor(offset[:, :], offset[:, :], p_pre[0:P, 0:NT], ALU.add)
                dve.tensor_scalar(chunk_no[:, :], chunk_no[:, :], end[:, 0:1], None, ALU.is_ge).then_inc(s_over, 1)
                dve.wait_ge(s_tile, 1)
                for k in range(4):
                    lo, hi = k * 512, min(k * 512 + 512, CH)
                    dve.tensor_scalar(tile_of[0:1, lo:hi], p_tile[k][0:1, 0:hi - lo], float(NT - 1), None, ALU.min)
                dve.drain()
                with dve.Fori(0, NT) as b:
                    dve.tensor_scalar(mask[:, :], tile16[:, :], m.count_t[:, bass.ds(b, 1)], None, ALU.is_equal)
                    dve.drain()
                    dve.tensor_tensor_scan(running[:, :], one16[:, :], mask[:, :], offset[:, bass.ds(b, 1)],
                                           ALU.mult, ALU.add)
                    dve.drain()
                    dve.copy_predicated(slot_f[:, :], mask[:, :].bitcast(I16), running[:, :])
                    dve.drain()
                dve.drain()
                dve.tensor_copy(tile_i[:, :], slot_f[:, :])
                dve.drain()
                dve.tensor_scalar(key_i[:, :], tile_i[:, :], LANES - 1, None, ALU.bitwise_and)
                dve.tensor_scalar(row_i[0][:, :], tile_i[:, :], 7, None, ALU.arith_shift_right)
                dve.drain()
                dve.scalar_tensor_tensor(out=pi[:, :, 0], in0=key_i[:, :], scalar=float(CH), in1=row_i[0][:, :],
                                         op0=ALU.mult, op1=ALU.add)

            @block.tensor
            def _(pe):
                pe.wait_ge(s_count, 1)
                pe.matmul(p_pre[0:P, 0:NT], m.below[:, :], count[:, :], start=True, stop=True)
                pe.matmul(p_tot[0:NT, 0:1], count[:, :], m.ones[0:P, 0:1], start=True, stop=True).then_inc(s_tot, 1)
                pe.wait_ge(s_n, 1)
                pe.matmul(p_start[0:P, 0:NT], n_wide[:, :], m.below[0:NT, 0:NT], start=True, stop=True)
                pe.matmul(p_end[0:NT, 0:1], upto[:, :], n_col[:, :], start=True, stop=True).then_inc(s_sum, 1)
                pe.wait_ge(s_over, 1)
                for k in range(4):
                    lo, hi = k * 512, min(k * 512 + 512, CH)
                    mm = pe.matmul(p_tile[k][0:1, 0:hi - lo], m.ones[0:NT, 0:1], chunk_no[:, lo:hi],
                                   start=True, stop=True)
                mm.then_inc(s_tile, 1)

            @block.scalar
            def _(act):
                act.wait_ge(m.s_chunk, 1)
                act.copy(chunk_no[:, :], m.chunk_i[:, :]).then_inc(s_iota, 1)


SG = 16
NS = EC // SG


def scatter_job(m, pi, slots, stage, name):
    s_scat = [m.sem(f"s_scat{u}_{name}") for u in range(2)]

    def job(pool):
        pool.wait_ge(m.s_fill, m.filled[name])

        def step(n, u):
            if later(n):
                pool.wait_ge(s_scat[u], (n - u) * (SG * 8))
            pool.tensor_copy(stage[u][:, :, :], pi[:, bass.ds(n * SG, SG), :])
            pool.drain()
            for k in range(SG):
                pool.indirect_dma_start(out=slots, out_offset=bass.IndirectOffsetOnAxis(ap=stage[u][:, k, 0:1], axis=0),
                                        in_=stage[u][:, k, 1:2], in_offset=None).then_inc(s_scat[u], 16)

        in_units(pool, step, NS)
        for u in range(2):
            pool.wait_ge(s_scat[u], NS // 2 * SG * 16)

    return job


def fill_slots(nc, m, slots_list):
    with ExitStack() as ctx:
        sb, ps, sem = m.scope(nc, ctx)
        empty = sb("empty", [LANES, CH], I32)
        s_empty = sem("s_empty")
        m.s_chunk = m.sem("s_chunk")
        m.s_fill = m.sem("s_fill")
        with m.block() as block:
            @block.vector
            def _(dve):
                dve.memset(empty[:, :], N * LANES + NOBODY).then_inc(s_empty, 1)

            @block.gpsimd
            def _(pool):
                pool.iota(m.chunk_i[:, :], [[1, CH]], base=0, channel_multiplier=0).then_inc(m.s_chunk, 1)

            @block.sync
            def _(sp):
                sp.wait_ge(s_empty, 1)
                for slots in slots_list:
                    sp.dma_start(slots.rearrange("(l c) o -> l (c o)", c=CH), empty[:, :]).then_inc(m.s_fill, 16)
                sp.wait_ge(m.s_fill, 16 * len(slots_list))
        m.filled = {"dst": 16 * len(slots_list), "src": 16 * len(slots_list)}



class Together:

    def __init__(self):
        self.parts = {k: [] for k in ("sync", "scalar", "vector", "tensor")}
        self.at = -1

    def __enter__(self):
        self.at += 1
        for k in self.parts:
            self.parts[k].append(None)
        return self

    def __exit__(self, *e):
        return False

    def sync(self, f):
        self.parts["sync"][self.at] = f

    def scalar(self, f):
        self.parts["scalar"][self.at] = f

    def vector(self, f):
        self.parts["vector"][self.at] = f

    def tensor(self, f):
        self.parts["tensor"][self.at] = f

    def run(self, nc, m, pool_job):
        s_met = m.sem(f"s_met{m.next_block()}")

        def all_of(eng, fs):
            for k, f in enumerate(fs):
                if f is not None:
                    f(eng)
                eng.drain().then_inc(s_met, 1)
                eng.wait_ge(s_met, 4 * (k + 1))

        with nc.Block() as block:
            @block.sync
            def _(sp):
                all_of(sp, self.parts["sync"])

            @block.scalar
            def _(act):
                all_of(act, self.parts["scalar"])

            @block.vector
            def _(dve):
                all_of(dve, self.parts["vector"])

            @block.tensor
            def _(pe):
                all_of(pe, self.parts["tensor"])

            @block.gpsimd
            def _(pool):
                pool_job(pool)



def in_pairs(eng, body):
    body(0)
    with eng.Fori(1, NT // 2) as i:
        body(i)


def not_first(i):
    return not isinstance(i, int)


def mix_query(nc, m, a, msg):
    with ExitStack() as ctx:
        sb, ps, sem = m.scope(nc, ctx)
        w_q, w_m = sb("mq_w_q", [128, 2, C], F32), sb("mq_w_m", [128, 2, C], F32)
        kv = sb("mq_kv", [128, 2, 132], F32)
        xn = sb("mq_xn", [P, 2, C], F32)
        xt = sb("mq_xt", [128, 2, 2, P], F32)
        qmin = sb("mq_qmin", [128, 2, 2 * P], F32)
        qf = sb("mq_qf", [128, 2, 2 * P], F32)
        z = sb("mq_z", [P, 2, 2, 4], F32)
        mn = sb("mq_mn", [P, 2, C], F32)
        mt = sb("mq_mt", [128, 2, 2, P], F32)
        p_t, p_q, p_mt, p_o = (ps(x, [128, 512]) for x in ("mq_p_t", "mq_p_q", "mq_p_mt", "mq_p_o"))
        p_m = [ps(f"mq_p_m{j}", [128, 512]) for j in range(2)]
        s_w, s_xn, s_tr, s_xt, s_q, s_min, s_exp, s_qf, s_num, s_mn, s_tm, s_mt, s_o, s_done = (sem("mq_" + x) for x in (
            "s_w", "s_xn", "s_tr", "s_xt", "s_q", "s_min", "s_exp", "s_qf", "s_num", "s_mn", "s_tm", "s_mt", "s_o",
            "s_done"))
        with m.block() as block:
            @block.sync
            def _(sp):
                sp.dma_start(w_q[:, :, :], a["L0_mix_Wq"].rearrange("(c p) n -> p c n", p=128)).then_inc(s_w, 16)
                sp.dma_start(w_m[:, :, :], a["L0_mix_Wm"].rearrange("(c p) n -> p c n", p=128)).then_inc(s_w, 16)

            @block.scalar
            def _(act):
                def step(i):
                    if not_first(i):
                        act.wait_ge(s_done, i)
                    for j in range(2):
                        ins = act.activation(xn[:, j, :], m.x[:, i * 2 + j, :], ACT.Identity,
                                             scale=m.rstd[:, bass.ds(i * 2 + j, 1)], bias=m.nmr[:, bass.ds(i * 2 + j, 1)])
                    ins.then_inc(s_xn, 1)
                    act.wait_ge(s_tr, i + 1)
                    act.copy(xt[:, :, :, :].rearrange("p c j n -> p (c j n)"), p_t[:, 0:4 * P]).then_inc(s_xt, 1)
                    act.wait_ge(s_min, i + 1)
                    act.activation(qf[:, :, :], qmin[:, :, :], ACT.Exp).then_inc(s_exp, 1)
                    act.wait_ge(s_tm, i + 1)
                    act.copy(mt[:, :, :, :].rearrange("p c j n -> p (c j n)"), p_mt[:, 0:4 * P]).then_inc(s_mt, 1)
                    act.wait_ge(s_o, i + 1)
                    act.copy(msg[:, bass.ds(i * 2, 2), :].rearrange("p j c -> p (j c)"), p_o[0:P, :]).then_inc(s_done, 1)

                in_pairs(act, step)

            @block.vector
            def _(dve):
                dve.memset(kv[:, :, :], 0.0)
                dve.drain()
                for g in range(2):
                    for h in range(4):
                        r = slice(32 * h, 32 * h + 32)
                        dve.tensor_copy(kv[r, g, 32 * h:32 * h + 32], m.kv_sum[r, 129 * g + 32 * h:129 * g + 32 * h + 32])
                        dve.tensor_copy(kv[r, g, 128 + h:129 + h], m.kv_sum[r, 129 * g + 128:129 * g + 129])
                dve.drain()

                def step(i):
                    dve.wait_ge(s_q, i + 1)
                    q = p_q[:, 0:4 * P].rearrange("p (o n) -> p o n", o=2)
                    dve.tensor_scalar(qmin[:, :, :], q, 0.0, None, ALU.min).then_inc(s_min, 1)
                    dve.wait_ge(s_exp, i + 1)
                    dve.scalar_tensor_tensor(out=qf[:, :, :], in0=q, scalar=0.0, in1=qf[:, :, :],
                                             op0=ALU.max, op1=ALU.add).then_inc(s_qf, 1)
                    dve.wait_ge(s_num, i + 1)
                    for j in range(2):
                        den = p_m[j][0:P, 0:264].rearrange("p (g v) -> p g v", g=2)[:, :, 128:132]
                        dve.tensor_scalar(z[:, j, :, :], den, 1e-6, None, ALU.add)
                    dve.drain()
                    dve.reciprocal(z[:, :, :, :], z[:, :, :, :])
                    dve.drain()
                    for j in range(2):
                        for g in range(2):
                            ins = dve.tensor_tensor(
                                mn[:, j, 128 * g:128 * g + 128].rearrange("p (h v) -> p h v", h=4),
                                p_m[j][0:P, 132 * g:132 * g + 128].rearrange("p (h v) -> p h v", h=4),
                                z[:, j, g, :].unsqueeze(2).broadcast_to((P, 4, 32)), ALU.mult)
                    ins.then_inc(s_mn, 1)

                in_pairs(dve, step)

            @block.tensor
            def _(pe):
                pe.wait_ge(s_w, 32)

                def step(i):
                    pe.wait_ge(s_xn, i + 1)
                    for c in range(2):
                        for j in range(2):
                            at = (2 * c + j) * P
                            mm = pe.transpose(p_t[:, at:at + P], xn[:, j, 128 * c:128 * c + 128], m.ident[0:P, 0:P])
                    mm.then_inc(s_tr, 1)
                    pe.wait_ge(s_xt, i + 1)
                    for o in range(2):
                        for c in range(2):
                            mm = pe.matmul(p_q[:, 2 * P * o:2 * P * o + 2 * P], w_q[:, c, 128 * o:128 * o + 128],
                                           xt[:, c, :, :].rearrange("p j n -> p (j n)"), start=c == 0, stop=c == 1)
                    mm.then_inc(s_q, 1)
                    pe.wait_ge(s_qf, i + 1)
                    for j in range(2):
                        for g in range(2):
                            mm = pe.matmul(p_m[j][0:P, 132 * g:132 * g + 132], qf[:, g, P * j:P * j + P], kv[:, g, :],
                                           start=True, stop=True)
                    mm.then_inc(s_num, 1)
                    pe.wait_ge(s_mn, i + 1)
                    for c in range(2):
                        for j in range(2):
                            at = (2 * c + j) * P
                            mm = pe.transpose(p_mt[:, at:at + P], mn[:, j, 128 * c:128 * c + 128], m.ident[0:P, 0:P])
                    mm.then_inc(s_tm, 1)
                    pe.wait_ge(s_mt, i + 1)
                    for j in range(2):
                        for c in range(2):
                            mm = pe.matmul(p_o[0:P, C * j:C * j + C], mt[:, c, j, :], w_m[:, c, :],
                                           start=c == 0, stop=c == 1)
                    mm.then_inc(s_o, 1)

                in_pairs(pe, step)


def mix_mlp(nc, m, a, msg, rstd, nmr):
    with ExitStack() as ctx:
        sb, ps, sem = m.scope(nc, ctx)
        w1 = sb("mm_w1", [128, 4, 2 * C], F32)
        w2 = sb("mm_w2", [128, 4, C], F32)
        gb = sb("mm_gb", [128, 2, 2], F32)
        xn = sb("mm_xn", [P, 2, 2, C], F32)
        zt = sb("mm_zt", [128, 4, 2 * P], F32)
        ht = sb("mm_ht", [128, 4, 2 * P], F32)
        p_t = [ps(f"mm_p_t{k}", [128, 512]) for k in range(2)]
        p_h = [ps(f"mm_p_h{k}", [128, 512]) for k in range(2)]
        p_y = ps("mm_p_y", [128, 512])
        s_w, s_xn, s_tr, s_zx, s_zm, s_h, s_relu, s_y, s_done = (sem("mm_" + x) for x in (
            "s_w", "s_xn", "s_tr", "s_zx", "s_zm", "s_h", "s_relu", "s_y", "s_done"))
        with m.block() as block:
            @block.sync
            def _(sp):
                sp.dma_start(w1[:, :, :], a["L0_mix_W1"].rearrange("(c p) n -> p c n", p=128)).then_inc(s_w, 16)
                sp.dma_start(w2[:, :, :], a["L0_mix_W2"].rearrange("(c p) n -> p c n", p=128)).then_inc(s_w, 16)
                for c in range(2):
                    sp.dma_start(gb[:, 0, c:c + 1], a["L0_mix_g1"][128 * c:128 * c + 128].rearrange("(p o) -> p o", o=1)).then_inc(s_w, 16)
                    sp.dma_start(gb[:, 1, c:c + 1], a["L0_mix_b1"][128 * c:128 * c + 128].rearrange("(p o) -> p o", o=1)).then_inc(s_w, 16)

            @block.scalar
            def _(act):
                def step(i):
                    if not_first(i):
                        act.wait_ge(s_done, i)
                    for j in range(2):
                        n = i * 2 + j
                        act.activation(xn[:, j, 0, :], m.x[:, n, :], ACT.Identity,
                                       scale=m.rstd[:, bass.ds(n, 1)], bias=m.nmr[:, bass.ds(n, 1)])
                        ins = act.activation(xn[:, j, 1, :], msg[:, n, :], ACT.Identity,
                                             scale=rstd[:, bass.ds(n, 1)], bias=nmr[:, bass.ds(n, 1)])
                    ins.then_inc(s_xn, 1)
                    act.wait_ge(s_tr, i + 1)
                    act.copy(zt[:, 0:2, :].rearrange("p c n -> p (c n)"), p_t[0][:, 0:4 * P]).then_inc(s_zx, 1)
                    act.wait_ge(s_h, i + 1)
                    for k in range(2):
                        ins = act.activation(ht[:, 2 * k:2 * k + 2, :].rearrange("p c n -> p (c n)"), p_h[k][:, 0:4 * P],
                                             ACT.Relu)
                    ins.then_inc(s_relu, 1)

                in_pairs(act, step)

            @block.vector
            def _(dve):
                dve.wait_ge(s_w, 96)

                def step(i):
                    dve.wait_ge(s_tr, i + 1)
                    for c in range(2):
                        ins = dve.tensor_scalar(zt[:, 2 + c, :], p_t[1][:, 2 * P * c:2 * P * c + 2 * P], gb[:, 0, c:c + 1],
                                                gb[:, 1, c:c + 1], ALU.mult, ALU.add)
                    ins.then_inc(s_zm, 1)
                    dve.wait_ge(s_y, i + 1)
                    dve.tensor_copy(msg[:, bass.ds(i * 2, 2), :].rearrange("p j c -> p (j c)"), p_y[0:P, :]).then_inc(s_done, 1)

                in_pairs(dve, step)

            @block.tensor
            def _(pe):
                pe.wait_ge(s_w, 96)

                def step(i):
                    pe.wait_ge(s_xn, i + 1)
                    for k in range(2):
                        for c in range(2):
                            for j in range(2):
                                at = (2 * c + j) * P
                                mm = pe.transpose(p_t[k][:, at:at + P], xn[:, j, k, 128 * c:128 * c + 128],
                                                  m.ident[0:P, 0:P])
                    mm.then_inc(s_tr, 1)
                    pe.wait_ge(s_zx, i + 1)
                    pe.wait_ge(s_zm, i + 1)
                    for o in range(4):
                        for c in range(4):
                            at = 2 * P * (o % 2)
                            mm = pe.matmul(p_h[o // 2][:, at:at + 2 * P], w1[:, c, 128 * o:128 * o + 128], zt[:, c, :],
                                           start=c == 0, stop=c == 3)
                    mm.then_inc(s_h, 1)
                    pe.wait_ge(s_relu, i + 1)
                    for j in range(2):
                        for c in range(4):
                            mm = pe.matmul(p_y[0:P, C * j:C * j + C], ht[:, c, P * j:P * j + P], w2[:, c, :],
                                           start=c == 0, stop=c == 3)
                    mm.then_inc(s_y, 1)

                in_pairs(pe, step)


def mix_add(nc, m, a, msg, rstd, nmr):
    with ExitStack() as ctx:
        sb, ps, sem = m.scope(nc, ctx)
        gb = sb("ma_gb", [P, 2, C], F32)
        xn = [sb(f"ma_xn{u}", [P, C], F32) for u in range(2)]
        hn = [sb(f"ma_hn{u}", [P, C], F32) for u in range(2)]
        s_w, s_n, s_used = (sem("ma_" + x) for x in ("s_w", "s_n", "s_used"))
        with m.block() as block:
            @block.sync
            def _(sp):
                sp.dma_start(gb[:, 0, :], a["L0_mix_g2"].rearrange("(o c) -> o c", o=1).broadcast_to((P, C))).then_inc(s_w, 16)
                sp.dma_start(gb[:, 1, :], a["L0_mix_b2"].rearrange("(o c) -> o c", o=1).broadcast_to((P, C))).then_inc(s_w, 16)

            @block.scalar
            def _(act):
                def step(n, u):
                    if later(n):
                        act.wait_ge(s_used, n - 1)
                    act.activation(xn[u][:, :], m.x[:, n, :], ACT.Identity, scale=m.rstd[:, bass.ds(n, 1)],
                                   bias=m.nmr[:, bass.ds(n, 1)])
                    act.activation(hn[u][:, :], msg[:, n, :], ACT.Identity, scale=rstd[:, bass.ds(n, 1)],
                                   bias=nmr[:, bass.ds(n, 1)]).then_inc(s_n, 1)

                in_units(act, step, NT)

            @block.vector
            def _(dve):
                dve.wait_ge(s_w, 32)

                def step(n, u):
                    dve.wait_ge(s_n, n + 1)
                    dve.tensor_tensor(hn[u][:, :], hn[u][:, :], gb[:, 0, :], ALU.mult)
                    dve.tensor_tensor(xn[u][:, :], xn[u][:, :], gb[:, 1, :], ALU.add)
                    dve.drain()
                    dve.tensor_tensor(hn[u][:, :], hn[u][:, :], xn[u][:, :], ALU.add)
                    dve.drain()
                    dve.tensor_tensor(m.x[:, n, :], m.x[:, n, :], hn[u][:, :], ALU.add).then_inc(s_used, 1)

                in_units(dve, step, NT)


def in_groups(eng, body, w=2):
    for u in range(w):
        body(u, u, False)
    k = (NG - 3) // w
    with eng.Fori(1, k) as i:
        for u in range(w):
            body(i * w + u, u, False)
    for n in range(k * w, NG):
        body(n, n % w, n == NG - 1)


def rounds(n, u, each):
    return (n // 2 + 1) * each if isinstance(n, int) else (n - u) * (each // 2) + each


def tiles_of(nc, engine, tile_of, n):
    return nc.values_load_multi_w_load_instructions(tile_of[0:1, bass.ds(n * G, G)], engines=[engine],
                                                    min_val=0, max_val=NT - 1)[1]


def load_slots(nc, m, slots, row_i, node_f, name):
    s_slots, s_node = m.sem(f"s_slots_{name}"), m.sem(f"s_node_{name}")
    with m.block() as block:
        @block.sync
        def _(sp):
            sp.dma_start(row_i[:, 0:CH], slots.rearrange("(l c) o -> l (c o)", c=CH)).then_inc(s_slots, 16)

        @block.vector
        def _(dve):
            dve.memset(row_i[:, CH:CH + G], 0)
            dve.wait_ge(s_slots, 16)
            dve.tensor_scalar(node_f[:, :].bitcast(I32), row_i[:, 0:CH], LANES - 1, None, ALU.bitwise_and)
            dve.drain()
            dve.tensor_copy(node_f[:, :], node_f[:, :].bitcast(I32))
            dve.tensor_scalar(row_i[:, 0:CH], row_i[:, 0:CH], 7, None, ALU.arith_shift_right)


def score_bounds(nc, m, acc, smax):
    with ExitStack() as ctx:
        sb, ps, sem = m.scope(nc, ctx)
        top = sb("sb_top", [P, H], F32)
        s_top, s_all = sem("sb_s_top"), sem("sb_s_all")
        bound = m.score[:, :, 0:H]
        with m.block() as block:
            @block.vector
            def _(dve):
                dve.memset(acc[:, :, :], 0.0)
                dve.memset(smax[:, :], NEG)
                dve.tensor_reduce(top[:, :], bound.rearrange("p t h -> p h t"), AX.X, ALU.max).then_inc(s_top, 1)
                dve.wait_ge(s_all, 1)
                dve.tensor_tensor(bound, m.score[:, :, H:2 * H], top[:, :].unsqueeze(1).broadcast_to((P, NT, H)), ALU.add)
                dve.drain()
                dve.scalar_tensor_tensor(out=bound, in0=bound, scalar=0.2, in1=bound, op0=ALU.mult, op1=ALU.max)

            @block.gpsimd
            def _(pool):
                pool.wait_ge(s_top, 1)
                pool.partition_all_reduce(top[:, :], top[:, :], P, RMAX).then_inc(s_all, 1)


def attend(nc, m, row_i, node_f, acc, smax):
    with ExitStack() as ctx:
        sb, ps, sem = m.scope(nc, ctx)
        stage = [sb(f"at_stage{u}", [128, G], I32) for u in range(4)]
        rows = [sb(f"at_rows{u}", [128, G, TW], F32) for u in range(2)]
        hot = [sb(f"at_hot{u}", [128, G, P], F32) for u in range(3)]
        hot_t = sb("at_hot_t", [P, G, 128], F32)
        zs = sb("at_zs", [128, G, H], F32)
        diff = sb("at_diff", [128, G, H], F32)
        near = [sb(f"at_near{u}", [P, G, 2 * H], F32) for u in range(2)]
        p_t = [ps(f"at_p_t{k}", [128, 512]) for k in range(2)]
        p_f = [ps(f"at_p_f{k}", [128, 512]) for k in range(2)]
        p_a = [ps(f"at_p_a{k}", [128, 512]) for k in range(4)]
        s_gath = [sem(f"at_s_gath{u}") for u in range(2)]
        s_stage, s_near, s_hot, s_t, s_hot_t, s_fetch, s_diff, s_exp, s_msg, s_agg, s_acc = (sem("at_" + x) for x in (
            "s_stage", "s_near", "s_hot", "s_t", "s_hot_t", "s_fetch", "s_diff", "s_exp", "s_msg", "s_agg", "s_acc"))
        parts = [(q, list(range(4 * q, min(4 * q + 4, G)))) for q in range((G + 3) // 4)]
        NQ = len(parts)
        with m.block() as block:
            @block.gpsimd
            def _(pool):
                pool.tensor_copy(stage[0][:, :], row_i[:, 0:G]).then_inc(s_stage, 1)

                def step(n, u, last):
                    if later(n):
                        pool.wait_ge(s_agg, n * G - G)
                    pool.wait_ge(s_stage, n + 1)
                    pool.tensor_copy(stage[(u + 1) % 4][:, :], row_i[:, bass.ds((n + 1) * G, G)]).then_inc(s_stage, 1)
                    for g in range(G):
                        pool.indirect_dma_start(out=rows[u % 2][:, g, :], out_offset=None, in_=m.table0,
                                                in_offset=bass.IndirectOffsetOnAxis(ap=stage[u][:, g:g + 1], axis=0)
                                                ).then_inc(s_gath[u % 2], 16)

                in_groups(pool, step, 4)

            @block.scalar
            def _(act):
                def copy_parts(n, some):
                    for q, gs in some:
                        act.wait_ge(s_t, n * NQ + q + 1)
                        act.copy(hot_t[:, gs[0]:gs[-1] + 1, :].rearrange("p g e -> p (g e)"),
                                 p_t[q % 2][0:P, 0:128 * len(gs)]).then_inc(s_hot_t, 1)

                def score_rows(n, u):
                    if later(n):
                        act.wait_ge(s_fetch, n - 1)
                    tiles = tiles_of(nc, mybir.EngineType.Activation, m.tile_dst, n)
                    for g in range(G):
                        act.copy(near[u][:, g, :], m.score[:, bass.ds(tiles[g], 1), :].rearrange("p o w -> p (o w)")
                                 ).then_inc(s_near, 1)

                score_rows(0, 0)
                score_rows(1, 1)
                copy_parts(0, parts)
                copy_parts(1, parts)
                score_rows(2, 0)

                def step(n, u, last):
                    end = lambda k: isinstance(n, int) and n + k >= NG
                    act.wait_ge(s_diff, n + 1)
                    act.activation(rows[u][:, :, C:TW], diff[:, :, :], ACT.Exp).then_inc(s_exp, 1)
                    if not end(2):
                        copy_parts(n + 2, parts[0:2])
                    if not end(3):
                        score_rows(n + 3, 1 - u)
                    if not end(2):
                        copy_parts(n + 2, parts[2:])

                in_groups(act, step)

            @block.vector
            def _(dve):
                def one_hot(n, v, gs):
                    k = len(gs)
                    dve.tensor_tensor(hot[v][:, gs[0]:gs[0] + k, :], m.count_p[:, :].unsqueeze(1).broadcast_to((128, k, P)),
                                      node_f[:, bass.ds(n * G + gs[0], k)].unsqueeze(2).broadcast_to((128, k, P)),
                                      ALU.is_equal).then_inc(s_hot, 1)

                for n in range(3):
                    for q, gs in parts:
                        one_hot(n, n, gs)

                def step(n, w, last):
                    u, v = w % 2, w % 3
                    f = p_f[u][:, 0:2 * H * G].rearrange("p (g s) -> p g s", g=G)
                    dve.wait_ge(s_fetch, n + 1)
                    dve.wait_ge(s_gath[u], rounds(n, u, 16 * G))
                    dve.tensor_tensor(zs[:, :, :], rows[u][:, :, C:TW], f[:, :, H:2 * H], ALU.add)
                    dve.drain()
                    dve.scalar_tensor_tensor(out=zs[:, :, :], in0=zs[:, :, :], scalar=0.2, in1=zs[:, :, :],
                                             op0=ALU.mult, op1=ALU.max)
                    dve.drain()
                    dve.tensor_tensor(diff[:, :, :], zs[:, :, :], f[:, :, 0:H], ALU.subtract).then_inc(s_diff, 1)
                    flat = zs[:, :, :].rearrange("p g h -> p (g h)")
                    dve.tensor_tensor(smax[:, :], smax[:, :], flat, ALU.max)
                    dve.wait_ge(s_exp, n + 1)
                    def scale_rows(q):
                        gs = parts[q][1]
                        part = rows[u][:, gs[0]:gs[-1] + 1, :]
                        dve.tensor_tensor(part[:, :, 0:C].rearrange("p g (h f) -> p g h f", h=H),
                                          part[:, :, 0:C].rearrange("p g (h f) -> p g h f", h=H),
                                          part[:, :, C:TW].unsqueeze(3).broadcast_to((128, len(gs), H, D)),
                                          ALU.mult).then_inc(s_msg, 1)

                    scale_rows(0)
                    scale_rows(1)
                    tiles = tiles_of(nc, mybir.EngineType.DVE, m.tile_dst, n)
                    for g in range(G):
                        if not (isinstance(n, int) and n == 0 and g == 0):
                            dve.wait_ge(s_acc, n * G + g)
                        dve.wait_ge(s_agg, n * G + g + 1)
                        row = acc[:, bass.ds(tiles[g], 1), :].rearrange("p o w -> p (o w)")
                        dve.tensor_tensor(row, row, p_a[g % 4][0:P, 0:TW], ALU.add).then_inc(s_acc, 1)
                        if g in (1, 3):
                            scale_rows(2 + g // 2)
                        for q, gs in parts:
                            if g == gs[-1] and not (isinstance(n, int) and n + 3 >= NG):
                                one_hot(n + 3, v, gs)

                in_groups(dve, step, 6)

            @block.tensor
            def _(pe):
                def turn(n, v, g):
                    if g % 4 == 0:
                        pe.wait_ge(s_hot, n * NQ + g // 4 + 1)
                        if not (isinstance(n, int) and n == 0 and g < 8):
                            pe.wait_ge(s_hot_t, n * NQ + g // 4 - 1)
                    mm = pe.transpose(p_t[g // 4 % 2][0:P, 128 * (g % 4):128 * (g % 4) + 128], hot[v][:, g, :], m.ident[:, :])
                    if g % 4 == 3 or g == G - 1:
                        mm.then_inc(s_t, 1)

                def fetch(n, u):
                    pe.wait_ge(s_hot_t, n * NQ + NQ)
                    pe.wait_ge(s_near, n * G + G)
                    if later(n):
                        pe.wait_ge(s_diff, n - 1)
                    for g in range(G):
                        mm = pe.matmul(p_f[u][:, 2 * H * g:2 * H * g + 2 * H], hot_t[:, g, :],
                                       near[u][:, g, :], start=True, stop=True)
                    mm.then_inc(s_fetch, 1)

                for n in range(2):
                    for g in range(G):
                        turn(n, n, g)
                    fetch(n, n)

                def step(n, w, last):
                    u, v = w % 2, w % 3
                    ahead = not (isinstance(n, int) and n + 2 >= NG)
                    if ahead:
                        for g in range(8):
                            turn(n + 2, (w + 2) % 3, g)
                    for g in range(G):
                        if g % 4 == 0:
                            pe.wait_ge(s_msg, n * NQ + g // 4 + 1)
                        if g >= 4:
                            pe.wait_ge(s_acc, n * G + g - 3)
                        elif g == 0 and not (isinstance(n, int) and n == 0):
                            pe.wait_ge(s_acc, n * G)
                        pe.matmul(p_a[g % 4][0:P, 0:TW], hot[v][:, g, :], rows[u][:, g, :],
                                  start=True, stop=True).then_inc(s_agg, 1)
                        if ahead and 3 <= g < 3 + G - 8:
                            turn(n + 2, (w + 2) % 3, g + 5)
                    if ahead:
                        fetch(n + 2, u)

                in_groups(pe, step, 6)


def attention_sums(nc, m, acc, smax, z):
    with ExitStack() as ctx:
        sb, ps, sem = m.scope(nc, ctx)
        top = sb("as_top", [128, 1], F32)
        s_top, s_all, s_gap, s_exp = (sem("as_" + x) for x in ("s_top", "s_all", "s_gap", "s_exp"))
        with nc.Block() as block:
            @block.vector
            def _(dve):
                dve.tensor_reduce(top[:, :], smax[:, :], AX.X, ALU.max).then_inc(s_top, 1)
                dve.wait_ge(s_all, 1)
                dve.tensor_scalar(z[:, :, :], m.score[:, :, 0:H], top[0:P, 0:1], -85.0, ALU.subtract, ALU.max).then_inc(s_gap, 1)
                dve.wait_ge(s_exp, 1)
                dve.scalar_tensor_tensor(out=z[:, :, :], in0=z[:, :, :], scalar=1e-16, in1=acc[:, :, C:TW],
                                         op0=ALU.mult, op1=ALU.add)
                dve.drain()
                dve.reciprocal(z[:, :, :], z[:, :, :])

            @block.gpsimd
            def _(pool):
                pool.wait_ge(s_top, 1)
                pool.partition_all_reduce(top[:, :], top[:, :], 128, RMAX).then_inc(s_all, 1)

            @block.scalar
            def _(act):
                act.wait_ge(s_gap, 1)
                act.activation(z[:, :, :], z[:, :, :], ACT.Exp, scale=-1.0).then_inc(s_exp, 1)


def attention_add(nc, m, a, acc, z):
    with ExitStack() as ctx:
        sb, ps, sem = m.scope(nc, ctx)
        bias = sb("aa_bias", [P, C], F32)
        skip = [sb(f"aa_skip{u}", [P, C], F32) for u in range(2)]
        y = [sb(f"aa_y{u}", [P, C], F32) for u in range(2)]
        low = [sb(f"aa_low{u}", [P, C], F32) for u in range(2)]
        s_b, s_low, s_exp, s_used = (sem("aa_" + x) for x in ("s_b", "s_low", "s_exp", "s_used"))
        s_skip = [sem(f"aa_s_skip{u}") for u in range(2)]
        with m.block() as block:
            @block.sync
            def _(sp):
                sp.dma_start(bias[:, :], a["L0_gnn_bias"].rearrange("(o c) -> o c", o=1).broadcast_to((P, C))).then_inc(s_b, 16)

                def step(n, u):
                    if later(n):
                        sp.wait_ge(s_used, n - 1)
                    sp.dma_start(skip[u][:, :], m.skip_rows[bass.ds(n * P, P), :]).then_inc(s_skip[u], 16)

                in_units(sp, step, NT)

            @block.scalar
            def _(act):
                def step(n, u):
                    act.wait_ge(s_low, n + 1)
                    act.activation(low[u][:, :], low[u][:, :], ACT.Exp).then_inc(s_exp, 1)

                in_units(act, step, NT)

            @block.vector
            def _(dve):
                dve.wait_ge(s_b, 16)

                def step(n, u):
                    dve.tensor_tensor(y[u][:, :].rearrange("p (h f) -> p h f", h=H),
                                      acc[:, bass.ds(n, 1), 0:C].rearrange("p o (h f) -> p (o h) f", h=H),
                                      z[:, bass.ds(n, 1), :].rearrange("p o h -> p (o h)").unsqueeze(2).broadcast_to((P, H, D)),
                                      ALU.mult)
                    dve.wait_ge(s_skip[u], rounds(n, u, 16))
                    dve.tensor_tensor(skip[u][:, :], skip[u][:, :], bias[:, :], ALU.add)
                    dve.drain()
                    dve.tensor_tensor(y[u][:, :], y[u][:, :], skip[u][:, :], ALU.add)
                    dve.drain()
                    dve.tensor_scalar(low[u][:, :], y[u][:, :], 0.0, None, ALU.min).then_inc(s_low, 1)
                    dve.wait_ge(s_exp, n + 1)
                    dve.scalar_tensor_tensor(out=y[u][:, :], in0=y[u][:, :], scalar=0.0, in1=low[u][:, :],
                                             op0=ALU.max, op1=ALU.add)
                    dve.drain()
                    dve.scalar_tensor_tensor(out=m.x[:, n, :], in0=y[u][:, :], scalar=-1.0, in1=m.x[:, n, :],
                                             op0=ALU.add, op1=ALU.add).then_inc(s_used, 1)

                in_units(dve, step, NT)


def slice_logits_weights(nc, m, a, w_log, b_log):
    with ExitStack() as ctx:
        sb, ps, sem = m.scope(nc, ctx)
        w_x = sb("sw_w_x", [128, 2, 512], F32)
        w_xt = sb("sw_w_xt", [128, 4, 256], F32)
        two = sb("sw_two", [128, 128], F32)
        b_x = sb("sw_b_x", [128, 4], F32)
        b_s = sb("sw_b_s", [1, SL], F32)
        temp = sb("sw_temp", [128, H], F32)
        p_t = [ps(f"sw_p_t{k}", [128, 512]) for k in range(2)]
        p_w = [ps(f"sw_p_w{k}", [128, 512]) for k in range(2)]
        p_b = ps("sw_p_b", [128, 512])
        s_zero, s_w, s_t, s_xt, s_p = (sem("sw_" + x) for x in ("s_zero", "s_w", "s_t", "s_xt", "s_p"))
        with m.block() as block:
            @block.sync
            def _(sp):
                sp.dma_start(w_x[:, :, :], a["L0_ffn_W_x"].rearrange("(c p) n -> p c n", p=128)).then_inc(s_w, 16)
                sp.dma_start(b_x[:, :], a["L0_ffn_b_x"].rearrange("(o p) -> p o", p=128), allow_slow_non_contiguous=True).then_inc(s_w, 16)
                sp.dma_start(b_s[:, :], a["L0_ffn_b_slice"].rearrange("(o p) -> o p", o=1)).then_inc(s_w, 16)
                sp.dma_start(temp[:, :], a["L0_ffn_temperature"].rearrange("a h b c -> a (h b c)").broadcast_to((128, H))).then_inc(s_w, 16)
                sp.wait_ge(s_zero, 1)
                for k in range(2):
                    sp.dma_start(two[64 * k:64 * k + 64, 64 * k:64 * k + 64], a["L0_ffn_W_slice"]).then_inc(s_w, 16)

            @block.vector
            def _(dve):
                dve.memset(two[:, :], 0.0).then_inc(s_zero, 1)
                dve.wait_ge(s_w, 96)
                dve.tensor_scalar(temp[:, :], temp[:, :], 0.1, 5.0, ALU.max, ALU.min)
                dve.drain()
                dve.reciprocal(temp[:, :], temp[:, :])
                dve.wait_ge(s_t, 1)
                for k in range(2):
                    ins = dve.tensor_copy(w_xt[:, 2 * k:2 * k + 2, :].rearrange("p o n -> p (o n)"), p_t[k][:, :])
                ins.then_inc(s_xt, 1)
                dve.wait_ge(s_p, 1)
                for c in range(2):
                    dve.tensor_tensor(w_log[:, c, :].rearrange("p (h g) -> p h g", h=H),
                                      p_w[c][:, :].rearrange("p (h g) -> p h g", h=H),
                                      temp[:, :].unsqueeze(2).broadcast_to((128, H, SL)), ALU.mult)
                b = b_log[0:1, :].rearrange("p (h g) -> p h g", h=H)
                dve.tensor_tensor(b, p_b[0:1, :].rearrange("p (h g) -> p h g", h=H),
                                  b_s[0:1, :].unsqueeze(1).broadcast_to((1, H, SL)), ALU.add)
                dve.drain()
                dve.tensor_tensor(b, b, temp[0:1, :].unsqueeze(2).broadcast_to((1, H, SL)), ALU.mult)

            @block.tensor
            def _(pe):
                pe.wait_ge(s_w, 96)
                for o in range(4):
                    for c in range(2):
                        at = 256 * (o % 2) + 128 * c
                        mm = pe.transpose(p_t[o // 2][:, at:at + 128], w_x[:, c, 128 * o:128 * o + 128], m.ident[:, :])
                mm.then_inc(s_t, 1)
                pe.wait_ge(s_xt, 1)
                for o in range(4):
                    for c in range(2):
                        pe.matmul(p_w[c][:, 128 * o:128 * o + 128], w_xt[:, o, 128 * c:128 * c + 128], two[:, :],
                                  start=True, stop=True)
                    mm = pe.matmul(p_b[0:1, 128 * o:128 * o + 128], b_x[:, o:o + 1], two[:, :], start=True, stop=True)
                mm.then_inc(s_p, 1)


def slice_weights(nc, m, w_log, b_log, swt, sx):
    with ExitStack() as ctx:
        sb, ps, sem = m.scope(nc, ctx)
        xn = [sb(f"sl_xn{u}", [P, C + 1], F32) for u in range(2)]
        xt = [sb(f"sl_xt{u}", [128, 2, P], F32) for u in range(2)]
        w = [sb(f"sl_w{u}", [P, H * SL], F32) for u in range(2)]
        top = sb("sl_top", [P, H], F32)
        total = sb("sl_total", [P, H], F32)
        p_s = [ps(f"sl_p_s{o}", [128, 512]) for o in range(4)]
        p_l = [ps(f"sl_p_l{u}", [128, 512]) for u in range(2)]
        p_t, p_w = ps("sl_p_t", [128, 512]), ps("sl_p_w", [128, 512])
        s_xn, s_tr, s_xt, s_log, s_sub, s_exp, s_sw, s_wt, s_swt, s_sum = (sem("sl_" + x) for x in (
            "s_xn", "s_tr", "s_xt", "s_log", "s_sub", "s_exp", "s_sw", "s_wt", "s_swt", "s_sum"))
        zero = sb("sl_zero", [128, C + 1], F32)
        s_zero = sem("sl_s_zero")
        with m.block() as block:
            @block.scalar
            def _(act):
                act.wait_ge(s_zero, 1)

                def front(n, u):
                    if later(n):
                        act.wait_ge(s_sum, n - 1)
                    act.activation(xn[u][:, 0:C], m.x[:, n, :], ACT.Identity, scale=m.rstd[:, bass.ds(n, 1)],
                                   bias=m.nmr[:, bass.ds(n, 1)]).then_inc(s_xn, 1)
                    act.wait_ge(s_tr, n + 1)
                    act.copy(xt[u][:, :, :].rearrange("p c n -> p (c n)"), p_t[:, 0:2 * P]).then_inc(s_xt, 1)

                front(0, 0)

                def step(n, u, last):
                    if not last:
                        front(n + 1, 1 - u)
                    act.wait_ge(s_sub, n + 1)
                    act.activation(w[u][:, :], w[u][:, :], ACT.Exp).then_inc(s_exp, 1)
                    act.wait_ge(s_wt, n + 1)
                    act.copy(swt[:, bass.ds(n, 1), :, :].rearrange("p a o n -> p (a o n)"), p_w[:, 0:4 * P]).then_inc(s_swt, 1)

                in_units_last(act, step)

            @block.vector
            def _(dve):
                for u in range(2):
                    dve.memset(xn[u][:, C:C + 1], 1.0)
                dve.memset(zero[:, :], 0.0)
                dve.drain().then_inc(s_zero, 1)

                def step(n, u):
                    dve.wait_ge(s_log, n + 1)
                    if later(n):
                        dve.wait_ge(s_sum, n - 1)
                    l = p_l[u][0:P, :].rearrange("p (h g) -> p h g", h=H)
                    e = w[u][:, :].rearrange("p (h g) -> p h g", h=H)
                    dve.tensor_reduce(top[:, :], l, AX.X, ALU.max)
                    dve.drain()
                    dve.tensor_tensor(e, l, top[:, :].unsqueeze(2).broadcast_to((P, H, SL)), ALU.subtract).then_inc(s_sub, 1)
                    dve.wait_ge(s_exp, n + 1)
                    dve.tensor_reduce(total[:, :], e, AX.X, ALU.add)
                    dve.drain()
                    dve.reciprocal(total[:, :], total[:, :])
                    dve.drain()
                    dve.tensor_tensor(e, e, total[:, :].unsqueeze(2).broadcast_to((P, H, SL)), ALU.mult).then_inc(s_sw, 1)

                in_units(dve, step, NT)
                dve.wait_ge(s_sum, NT)
                for o in range(4):
                    dve.tensor_copy(sx[:, o, :], p_s[o][:, 0:C + 1])

            @block.tensor
            def _(pe):
                pe.wait_ge(s_zero, 1)
                for o in range(4):
                    pe.matmul(p_s[o][:, 0:C + 1], zero[:, 0:128], zero[:, :], start=True, stop=False, skip_group_check=True)

                def front(n, u):
                    pe.wait_ge(s_xn, n + 1)
                    if not first(n):
                        pe.wait_ge(s_xt, n)
                    for c in range(2):
                        mm = pe.transpose(p_t[:, P * c:P * c + P], xn[u][:, 128 * c:128 * c + 128], m.ident[0:P, 0:P])
                    mm.then_inc(s_tr, 1)
                    pe.wait_ge(s_xt, n + 1)
                    if later(n):
                        pe.wait_ge(s_sub, n - 1)
                    for c in range(2):
                        pe.matmul(p_l[u][0:P, :], xt[u][:, c, :], w_log[:, c, :], start=c == 0, stop=False)
                    pe.matmul(p_l[u][0:P, :], m.ones[0:1, 0:P], b_log[0:1, :], start=False, stop=True).then_inc(s_log, 1)

                front(0, 0)

                def step(n, u, last):
                    if not last:
                        front(n + 1, 1 - u)
                    pe.wait_ge(s_sw, n + 1)
                    if not first(n):
                        pe.wait_ge(s_swt, n)
                    for o in range(4):
                        mm = pe.transpose(p_w[:, P * o:P * o + P], w[u][:, 128 * o:128 * o + 128], m.ident[0:P, 0:P])
                    mm.then_inc(s_wt, 1)
                    for o in range(4):
                        mm = pe.matmul(p_s[o][:, 0:C + 1], w[u][:, 128 * o:128 * o + 128], xn[u][:, :],
                                       start=False, stop=False, skip_group_check=True)
                    mm.then_inc(s_sum, 1)

                in_units_last(pe, step)


def slice_attention(nc, m, a, sx, w_back):
    with ExitStack() as ctx:
        sb, ps, sem = m.scope(nc, ctx)
        first = sb("sa_first", [128, 2048], F32)
        w_fx = first[:, 0:1024].rearrange("p (c n) -> p c n", c=2)
        sxt = first[:, 1024:2048].rearrange("p (c o g) -> p c o g", c=2, o=4)
        w_out = first[0:64, :].rearrange("p (h n) -> p h n", h=H)
        w_qkv = sb("sa_w_qkv", [64, 3, 64], F32)
        z = sb("sa_z", [64, H], F32)
        tok = sb("sa_tok", [64, 512], F32)
        tok_t = sb("sa_tok_t", [64, 512], F32)
        qt, kt, v = sb("sa_qt", [64, 512], F32), sb("sa_kt", [64, 512], F32), sb("sa_v", [64, 512], F32)
        att, att_t, ost = tok, tok_t, qt
        b_fx, norm = v[0:1, :], kt[0:1, :]
        b = [ps(f"sa_b{k}", [128, 512]) for k in range(8)]
        s_w, s_w_out, s_pe, s_dve, s_exp = (sem("sa_" + x) for x in ("s_w", "s_w_out", "s_pe", "s_dve", "s_exp"))
        heads = lambda x: x.rearrange("p (h g) -> p h g", h=H)
        wide = lambda x: x.unsqueeze(2).broadcast_to((64, H, 64))
        with m.block() as block:
            @block.sync
            def _(sp):
                sp.dma_start(w_fx[:, :, :], a["L0_ffn_W_fx"].rearrange("(c p) n -> p c n", p=128)).then_inc(s_w, 16)
                sp.dma_start(b_fx[:, :], a["L0_ffn_b_fx"].rearrange("(o n) -> o n", o=1)).then_inc(s_w, 16)
                for k, w in enumerate((a["L0_ffn_W_q"], a["L0_ffn_W_k"], a["L0_ffn_W_v"])):
                    sp.dma_start(w_qkv[:, k, :], w).then_inc(s_w, 16)
                sp.wait_ge(s_pe, 2)
                sp.dma_start(w_out[:, :, :], a["L0_ffn_W_out"].rearrange("(h c) n -> c h n", c=64)).then_inc(s_w_out, 16)

            @block.tensor
            def _(pe):
                pe.wait_ge(s_w, 80)
                for c in range(2):
                    for o in range(4):
                        pe.transpose(b[c][:, 128 * o:128 * o + 128], sx[:, o, 128 * c:128 * c + 128], m.ident[:, :])
                for o in range(4):
                    mm = pe.transpose(b[2][0:1, 128 * o:128 * o + 128], sx[:, o, C:C + 1], m.ident[:, :])
                mm.then_inc(s_pe, 1)
                pe.wait_ge(s_dve, 1)
                for h in range(H):
                    r = slice(64 * h, 64 * h + 64)
                    for c in range(2):
                        pe.matmul(b[3][0:64, r], sxt[:, c, h // 2, 64 * (h % 2):64 * (h % 2) + 64], w_fx[:, c, r],
                                  start=c == 0, stop=False)
                    pe.matmul(b[3][0:64, r], norm[0:1, r], b_fx[0:1, r], start=False, stop=True)
                for h in range(H):
                    mm = pe.matmul(b[4][0:64, h:h + 1], norm[0:1, 64 * h:64 * h + 64], m.ones[0:1, 0:1], start=True, stop=True)
                mm.then_inc(s_pe, 1)
                pe.wait_ge(s_dve, 2)
                for h in range(H):
                    mm = pe.transpose(b[5][0:64, 64 * h:64 * h + 64], tok[:, 64 * h:64 * h + 64], m.ident[0:64, 0:64])
                mm.then_inc(s_pe, 1)
                pe.wait_ge(s_dve, 3)
                pe.matmul(b[0][0:64, :], w_qkv[:, 0, :], tok_t[:, :], start=True, stop=True)
                pe.matmul(b[1][0:64, :], w_qkv[:, 1, :], tok_t[:, :], start=True, stop=True)
                for h in range(H):
                    mm = pe.matmul(b[2][0:64, 64 * h:64 * h + 64], tok_t[:, 64 * h:64 * h + 64], w_qkv[:, 2, :],
                                   start=True, stop=True)
                mm.then_inc(s_pe, 1)
                pe.wait_ge(s_dve, 4)
                for h in range(H):
                    r = slice(64 * h, 64 * h + 64)
                    mm = pe.matmul(b[3][0:64, r], qt[:, r], kt[:, r], start=True, stop=True)
                mm.then_inc(s_pe, 1)
                pe.wait_ge(s_dve, 5)
                for h in range(H):
                    r = slice(64 * h, 64 * h + 64)
                    mm = pe.transpose(b[4][0:64, r], att[:, r], m.ident[0:64, 0:64])
                mm.then_inc(s_pe, 1)
                pe.wait_ge(s_dve, 6)
                for h in range(H):
                    r = slice(64 * h, 64 * h + 64)
                    mm = pe.matmul(b[5][0:64, r], v[:, r], att_t[:, r], start=True, stop=True)
                mm.then_inc(s_pe, 1)
                pe.wait_ge(s_dve, 7)
                pe.wait_ge(s_w_out, 16)
                for h in range(H):
                    k = 64 * (h % 2)
                    o = h // 2
                    mm = pe.matmul(b[o // 2][k:k + 64, C * (o % 2):C * (o % 2) + C], ost[:, 64 * h:64 * h + 64],
                                   w_out[:, h, :], start=True, stop=True)
                mm.then_inc(s_pe, 1)

            @block.vector
            def _(dve):
                dve.wait_ge(s_pe, 1)
                for c in range(2):
                    dve.tensor_copy(sxt[:, c, :, :].rearrange("p o n -> p (o n)"), b[c][:, :])
                dve.tensor_copy(norm[:, :], b[2][0:1, :])
                dve.drain().then_inc(s_dve, 1)
                dve.wait_ge(s_pe, 2)
                dve.tensor_scalar(z[:, :], b[4][0:64, 0:H], 1e-5, None, ALU.add)
                dve.drain()
                dve.reciprocal(z[:, :], z[:, :])
                dve.drain()
                dve.tensor_tensor(heads(tok[:, :]), heads(b[3][0:64, :]), wide(z[:, :]), ALU.mult).then_inc(s_dve, 1)
                dve.wait_ge(s_pe, 3)
                dve.tensor_copy(tok_t[:, :], b[5][0:64, :]).then_inc(s_dve, 1)
                dve.wait_ge(s_pe, 4)
                for k, y in enumerate((qt, kt, v)):
                    dve.tensor_copy(y[:, :], b[k][0:64, :])
                dve.drain().then_inc(s_dve, 1)
                dve.wait_ge(s_pe, 5)
                dve.tensor_reduce(z[:, :], heads(b[3][0:64, :]), AX.X, ALU.max)
                dve.drain()
                dve.tensor_tensor(heads(att[:, :]), heads(b[3][0:64, :]), wide(z[:, :]), ALU.subtract)
                dve.drain().then_inc(s_exp, 1)
                dve.wait_ge(s_exp, 2)
                dve.tensor_reduce(z[:, :], heads(att[:, :]), AX.X, ALU.add)
                dve.drain()
                dve.reciprocal(z[:, :], z[:, :])
                dve.drain()
                dve.tensor_tensor(heads(att[:, :]), heads(att[:, :]), wide(z[:, :]), ALU.mult).then_inc(s_dve, 1)
                dve.wait_ge(s_pe, 6)
                dve.tensor_copy(att_t[:, :], b[4][0:64, :]).then_inc(s_dve, 1)
                dve.wait_ge(s_pe, 7)
                dve.tensor_copy(ost[:, :], b[5][0:64, :]).then_inc(s_dve, 1)
                dve.wait_ge(s_pe, 8)
                for k in range(2):
                    dve.tensor_copy(w_back[:, 2 * k:2 * k + 2, :].rearrange("p o n -> p (o n)"), b[k][:, :])

            @block.scalar
            def _(act):
                act.wait_ge(s_exp, 1)
                act.activation(att[:, :], att[:, :], ACT.Exp, scale=DS ** -0.5).then_inc(s_exp, 1)


def slice_add(nc, m, a, swt, w_back):
    with ExitStack() as ctx:
        sb, ps, sem = m.scope(nc, ctx)
        bias = sb("so_bias", [P, C], F32)
        st = [sb(f"so_st{u}", [128, 4, P], F32) for u in range(2)]
        p_o = [ps(f"so_p_o{u}", [128, 512]) for u in range(2)]
        s_b, s_st, s_o, s_x = (sem("so_" + x) for x in ("s_b", "s_st", "s_o", "s_x"))
        with m.block() as block:
            @block.sync
            def _(sp):
                sp.dma_start(bias[:, :], a["L0_ffn_b_out"].rearrange("(o c) -> o c", o=1).broadcast_to((P, C))).then_inc(s_b, 16)

            @block.scalar
            def _(act):
                def step(n, u):
                    if later(n):
                        act.wait_ge(s_o, n - 1)
                    act.copy(st[u][:, :, :].rearrange("p o n -> p (o n)"),
                             swt[:, bass.ds(n, 1), :, :].rearrange("p a o n -> p (a o n)")).then_inc(s_st, 1)

                in_units(act, step, NT)

            @block.tensor
            def _(pe):
                def step(n, u):
                    pe.wait_ge(s_st, n + 1)
                    if later(n):
                        pe.wait_ge(s_x, n - 1)
                    for o in range(4):
                        mm = pe.matmul(p_o[u][0:P, 0:C], st[u][:, o, :], w_back[:, o, :], start=o == 0, stop=o == 3)
                    mm.then_inc(s_o, 1)

                in_units(pe, step, NT)

            @block.vector
            def _(dve):
                dve.wait_ge(s_b, 16)

                def step(n, u):
                    dve.tensor_tensor(m.x[:, n, :], m.x[:, n, :], bias[:, :], ALU.add)
                    dve.drain()
                    dve.wait_ge(s_o, n + 1)
                    dve.tensor_tensor(m.x[:, n, :], m.x[:, n, :], p_o[u][0:P, 0:C], ALU.add).then_inc(s_x, 1)

                in_units(dve, step, NT)


def relation_table(nc, m, a):
    with ExitStack() as ctx:
        sb, ps, sem = m.scope(nc, ctx)
        w = sb("rt_w", [128, 2, R, C], F32)
        xn = [sb(f"rt_xn{u}", [P, C], F32) for u in range(2)]
        xt = [sb(f"rt_xt{u}", [128, 2, P], F32) for u in range(2)]
        row = [sb(f"rt_row{u}", [P, R, C], F32) for u in range(2)]
        p_t = [ps(f"rt_p_t{u}", [128, 512]) for u in range(2)]
        p_w = [ps(f"rt_p_w{k}", [128, 512]) for k in range(4)]
        s_w, s_xn, s_tr, s_xt, s_mm, s_even, s_odd = (sem("rt_" + x) for x in (
            "s_w", "s_xn", "s_tr", "s_xt", "s_mm", "s_even", "s_odd"))
        s_out = [sem(f"rt_s_out{u}") for u in range(2)]
        with m.block() as block:
            @block.sync
            def _(sp):
                for c in range(2):
                    sp.dma_start(w[:, c, :, :], a["L1_gnn_weight"][:, 128 * c:128 * c + 128, :].rearrange("r p o -> p r o")).then_inc(s_w, 16)

                def step(n, u):
                    sp.wait_ge(s_even, n + 1)
                    sp.wait_ge(s_odd, n + 1)
                    sp.dma_start(m.table1.rearrange("(r n) c -> n r c", r=R)[bass.ds(n * P, P), :, :],
                                 row[u][:, :, :]).then_inc(s_out[u], 16)

                in_units(sp, step, NT)
                for u in range(2):
                    sp.wait_ge(s_out[u], NT // 2 * 16)

            def copies(eng, copy, n, u, k0, s_copied):
                if later(n):
                    eng.wait_ge(s_out[u], rounds(n - 2, u, 16))
                for k in (k0, k0 + 2):
                    eng.wait_ge(s_mm, n * 4 + k + 1)
                    ins = copy(row[u][:, 2 * k:2 * k + 2, :].rearrange("p r c -> p (r c)"), p_w[k][0:P, :])
                ins.then_inc(s_copied, 1)

            @block.scalar
            def _(act):
                def norm(n, u):
                    if later(n):
                        act.wait_ge(s_tr, n - 1)
                    act.activation(xn[u][:, :], m.x[:, n, :], ACT.Identity, scale=m.rstd[:, bass.ds(n, 1)],
                                   bias=m.nmr[:, bass.ds(n, 1)]).then_inc(s_xn, 1)

                norm(0, 0)

                def step(n, u, last):
                    if not last:
                        norm(n + 1, 1 - u)
                    copies(act, act.copy, n, u, 0, s_even)

                in_units_last(act, step)

            @block.vector
            def _(dve):
                def copy_xt(n, u):
                    dve.wait_ge(s_tr, n + 1)
                    if later(n):
                        dve.wait_ge(s_mm, (n - 1) * 4)
                    dve.tensor_copy(xt[u][:, :, :].rearrange("p c n -> p (c n)"), p_t[u][:, 0:2 * P]).then_inc(s_xt, 1)

                copy_xt(0, 0)

                def step(n, u, last):
                    if not last:
                        copy_xt(n + 1, 1 - u)
                    copies(dve, dve.tensor_copy, n, u, 1, s_odd)

                in_units_last(dve, step)

            @block.tensor
            def _(pe):
                pe.wait_ge(s_w, 32)

                def turn(n, u):
                    pe.wait_ge(s_xn, n + 1)
                    if later(n):
                        pe.wait_ge(s_xt, n - 1)
                    for c in range(2):
                        mm = pe.transpose(p_t[u][:, P * c:P * c + P], xn[u][:, 128 * c:128 * c + 128], m.ident[0:P, 0:P])
                    mm.then_inc(s_tr, 1)

                turn(0, 0)

                def step(n, u, last):
                    if not last:
                        turn(n + 1, 1 - u)
                    pe.wait_ge(s_xt, n + 1)
                    if not (isinstance(n, int) and n == 0):
                        pe.wait_ge(s_even, n)
                        pe.wait_ge(s_odd, n)
                    for k in range(4):
                        for c in range(2):
                            mm = pe.matmul(p_w[k][0:P, :], xt[u][:, c, :],
                                           w[:, c, 2 * k:2 * k + 2, :].rearrange("p r o -> p (r o)"),
                                           start=c == 0, stop=c == 1)
                        mm.then_inc(s_mm, 1)

                in_units_last(pe, step)


SHIFTS = D // 2
HB = D + 1
HALF = 4 * HB
Q_SCALE = float(D) ** 0.25


def unit_rows(dve, root, rows, once, twice, guard_scale):
    dve.tensor_scalar(root, root, 1e-12, None, ALU.max)
    dve.drain()
    dve.reciprocal(root, root)
    dve.drain()
    if isinstance(guard_scale, float):
        dve.tensor_scalar(root, root, guard_scale, None, ALU.mult)
    else:
        dve.tensor_tensor(root, root, guard_scale, ALU.mult)
    dve.drain()
    z = root.unsqueeze(2).broadcast_to((P, H, D))
    half = root.unsqueeze(2).broadcast_to((P, H, D // 2))
    dve.tensor_tensor(twice[:, :, 0:D], rows, z, ALU.mult)
    dve.tensor_tensor(twice[:, :, D:D + D // 2], rows[:, :, 0:D // 2], half, ALU.mult)
    dve.tensor_tensor(once, rows, z, ALU.mult)
    dve.drain()


def shifted_products(dve, once, twice, prod, far):
    for s in range(SHIFTS + 1):
        out = prod[:, :, s, :] if s < SHIFTS else far
        ins = dve.tensor_tensor(out, once, twice[:, :, s:s + D], ALU.mult)
    return ins


def moments(nc, m, a, m_near, m_far, v_sum):
    with ExitStack() as ctx:
        sb, ps, sem = m.scope(nc, ctx)
        w = sb("mo_w", [128, 2, 2 * C], F32)
        b = sb("mo_b", [1, 2 * C], F32)
        xn = [sb(f"mo_xn{u}", [P, C], F32) for u in range(2)]
        xt = [sb(f"mo_xt{u}", [128, 2, P], F32) for u in range(2)]
        sq = sb("mo_sq", [P, C], F32)
        root = [sb(f"mo_root{u}", [P, H], F32) for u in range(2)]
        k2 = [sb(f"mo_k2{u}", [P, H, D + D // 2], F32) for u in range(2)]
        prod = [sb(f"mo_prod{u}", [P, H, SHIFTS, D], F32) for u in range(2)]
        far = [sb(f"mo_far{u}", [P, 2, H, D], F32) for u in range(2)]
        v1 = [sb(f"mo_v1{u}", [P, H, HB], F32) for u in range(2)]
        zero = sb("mo_zero", [128, 512], F32)
        near_t = sb("mo_near_t", [128, 4, 512], F32)
        p_t = ps("mo_p_t", [128, 512])
        p_kv = ps("mo_p_kv", [128, 512])
        p_n = [ps(f"mo_p_n{k}", [128, 512]) for k in range(4)]
        p_m = [ps(f"mo_p_m{k}", [128, 512]) for k in range(2)]
        s_w, s_xn, s_tr, s_xt, s_kv, s_sq, s_sum, s_root, s_v, s_prod, s_fold, s_zero, s_k, s_near, s_turn = (
            sem("mo_" + x) for x in (
            "s_w", "s_xn", "s_tr", "s_xt", "s_kv", "s_sq", "s_sum", "s_root", "s_v", "s_prod", "s_fold", "s_zero",
                                     "s_k", "s_near", "s_turn"))
        near = lambda h: p_n[h // 2][64 * (h % 2):64 * (h % 2) + HB, :]
        p_far = lambda g: p_m[0][:, HALF * g:HALF * g + HALF]
        p_lin = lambda g: p_m[1][:, HALF * g:HALF * g + HALF]
        p_one = lambda g: p_m[g][0:1, 2 * HALF:3 * HALF]
        heads = lambda x: x.rearrange("p (h f) -> p h f", h=H)
        with m.block() as block:
            @block.sync
            def _(sp):
                sp.dma_start(w[:, :, :], a["L1_mix_Wqkv"][:, C:3 * C].rearrange("(c p) n -> p c n", p=128)).then_inc(s_w, 16)
                sp.dma_start(b[:, :], a["L1_mix_bqkv"][C:3 * C].rearrange("(o n) -> o n", o=1)).then_inc(s_w, 16)

            @block.scalar
            def _(act):
                def step(n, u):
                    if later(n):
                        act.wait_ge(s_tr, n - 1)
                    act.activation(xn[u][:, :], m.x[:, n, :], ACT.Identity, scale=m.rstd[:, bass.ds(n, 1)],
                                   bias=m.nmr[:, bass.ds(n, 1)]).then_inc(s_xn, 1)
                    act.wait_ge(s_tr, n + 1)
                    if later(n):
                        act.wait_ge(s_kv, n - 1)
                    act.copy(xt[u][:, :, :].rearrange("p c n -> p (c n)"), p_t[:, 0:2 * P]).then_inc(s_xt, 1)
                    act.wait_ge(s_kv, n + 1)
                    if not (isinstance(n, int) and n == 0):
                        act.wait_ge(s_sum, n)
                    act.activation(sq[:, :], p_kv[0:P, 0:C], ACT.Square).then_inc(s_sq, 1)
                    if later(n):
                        act.wait_ge(s_fold, n - 1)
                    act.copy(v1[u][:, :, 1:HB], heads(p_kv[0:P, C:2 * C])).then_inc(s_v, 1)
                    act.wait_ge(s_sum, n + 1)
                    act.activation(root[u][:, :], root[u][:, :], ACT.Sqrt).then_inc(s_root, 1)

                in_units(act, step, NT)

            @block.vector
            def _(dve):
                for u in range(2):
                    dve.memset(v1[u][:, :, 0:1], 1.0)
                dve.memset(zero[:, :], 0.0)
                dve.memset(m_far[:, :, :, :], 0.0)
                dve.memset(near_t[:, :, :], 0.0)
                dve.drain().then_inc(s_zero, 1)

                def square_sum(n, u):
                    dve.wait_ge(s_sq, n + 1)
                    dve.tensor_reduce(root[u][:, :], heads(sq[:, :]), AX.X, ALU.add).then_inc(s_sum, 1)

                def step(n, u, last=False):
                    dve.wait_ge(s_root, n + 1)
                    if later(n):
                        dve.wait_ge(s_fold, n - 1)
                    unit_rows(dve, root[u][:, :], heads(p_kv[0:P, 0:C]), far[u][:, 1, :, :], k2[u], Q_SCALE)
                    dve.drain().then_inc(s_k, 1)
                    shifted_products(dve, far[u][:, 1, :, :], k2[u], prod[u], far[u][:, 0, :, :]).then_inc(s_prod, 1)
                    if not last:
                        square_sum(n + 1, 1 - u)

                square_sum(0, 0)
                for n in range(2):
                    step(n, n)
                with dve.Fori(1, NT // 2 - 1) as i:
                    for u in range(2):
                        step(i * 2 + u, u)
                for n in range(NT - 2, NT):
                    step(n, n % 2, n == NT - 1)
                dve.wait_ge(s_fold, NT)
                for k in range(4):
                    for r in (slice(0, HB), slice(64, 64 + HB)):
                        ins = dve.tensor_scalar(near_t[r, k, :], p_n[k][r, :], 1.0 / N, None, ALU.mult)
                ins.then_inc(s_near, 1)
                for k in range(4):
                    dve.wait_ge(s_turn, k + 1)
                    dve.tensor_copy(m_near[:, 8 * k:8 * k + 8, :].rearrange("p (q j) v -> p q j v", q=2),
                                    p_n[k][:, :].rearrange("p (j q w) -> p q j w", j=4, q=2)[:, :, :, 0:HB])
                dve.drain()
                own = m_near[0:D, :, :].rearrange("p (h q) v -> p h q v", q=4)[:, :, 0, :]
                dve.tensor_scalar(own, own, 0.5, None, ALU.mult)
                for h in range(H):
                    g, k = h // 4, h % 4
                    r = slice(D * k, D * k + D)
                    dve.tensor_scalar(m_far[r, 0, g, HB * k:HB * k + HB], p_far(g)[r, HB * k:HB * k + HB], 0.5 / N, None, ALU.mult)
                    dve.tensor_scalar(m_far[r, 1, g, HB * k:HB * k + HB], p_lin(g)[r, HB * k:HB * k + HB],
                                      Q_SCALE ** 2 / N, None, ALU.mult)
                for g in range(2):
                    dve.tensor_scalar(v_sum[0:1, g, :], p_one(g), Q_SCALE ** 4 / N, None, ALU.mult)

            @block.tensor
            def _(pe):
                pe.wait_ge(s_w, 32)
                pe.wait_ge(s_zero, 1)
                for p_z in p_n + p_m:
                    pe.matmul(p_z[:, :], zero[:, 0:128], zero[:, :], start=True, stop=False, skip_group_check=True)

                def front(n, u):
                    pe.wait_ge(s_xn, n + 1)
                    if not first(n):
                        pe.wait_ge(s_xt, n)
                    for c in range(2):
                        mm = pe.transpose(p_t[:, P * c:P * c + P], xn[u][:, 128 * c:128 * c + 128], m.ident[0:P, 0:P])
                    mm.then_inc(s_tr, 1)
                    pe.wait_ge(s_xt, n + 1)
                    if not first(n):
                        pe.wait_ge(s_k, n)
                        pe.wait_ge(s_v, n)
                    for c in range(2):
                        pe.matmul(p_kv[0:P, :], xt[u][:, c, :], w[:, c, :], start=c == 0, stop=False)
                    pe.matmul(p_kv[0:P, :], m.ones[0:1, 0:P], b[0:1, :], start=False, stop=True).then_inc(s_kv, 1)

                def fold(n, u):
                    pe.wait_ge(s_prod, n + 1)
                    pe.wait_ge(s_v, n + 1)
                    add = lambda out, l, r: pe.matmul(out, l, r, start=False, stop=False, skip_group_check=True)
                    for h in range(H):
                        add(near(h), v1[u][:, h, :], prod[u][:, h, :, :].rearrange("p s i -> p (s i)"))
                    for g in range(2):
                        half = v1[u][:, 4 * g:4 * g + 4, :].rearrange("p h v -> p (h v)")
                        add(p_far(g), far[u][:, 0, 4 * g:4 * g + 4, :].rearrange("p h i -> p (h i)"), half)
                        add(p_lin(g), far[u][:, 1, 4 * g:4 * g + 4, :].rearrange("p h i -> p (h i)"), half)
                        mm = add(p_one(g), m.ones[0:P, 0:1], half)
                    mm.then_inc(s_fold, 1)

                front(0, 0)
                front(1, 1)
                fold(0, 0)
                with pe.Fori(1, NT // 2) as i:
                    for u in range(2):
                        front(i * 2 + u, u)
                        fold(i * 2 + u - 1, 1 - u)
                fold(NT - 1, 1)
                pe.wait_ge(s_near, 1)
                for k in range(4):
                    for j in range(4):
                        mm = pe.transpose(p_n[k][:, 128 * j:128 * j + 128], near_t[:, k, 128 * j:128 * j + 128], m.ident[:, :])
                    mm.then_inc(s_turn, 1)


def quadratic_attention(nc, m, a, m_near, m_far, v_sum):
    with ExitStack() as ctx:
        sb, ps, sem = m.scope(nc, ctx)
        w_q = sb("qa_w_q", [128, 2, C], F32)
        b_q = sb("qa_b_q", [1, C], F32)
        w_p = sb("qa_w_p", [128, 2, C], F32)
        b_p = sb("qa_b_p", [1, C], F32)
        temp = sb("qa_temp", [P, H], F32)
        xn = sb("qa_xn", [P, C], F32)
        xt = sb("qa_xt", [128, 2, P], F32)
        sq = sb("qa_sq", [P, C], F32)
        root = sb("qa_root", [P, H], F32)
        q2 = [sb(f"qa_q2{u}", [P, H, D + D // 2], F32) for u in range(2)]
        prod = [sb(f"qa_prod{u}", [P, H, SHIFTS, D], F32) for u in range(2)]
        far = [sb(f"qa_far{u}", [P, 2, H, D], F32) for u in range(2)]
        part = [sb(f"qa_part{k}", [128, 4, P], F32) for k in range(3)]
        z = sb("qa_z", [P, H], F32)
        y = sb("qa_y", [P, C], F32)
        yt = sb("qa_yt", [128, 2, P], F32)
        p_q = ps("qa_p_q", [128, 512])
        p_c = [ps(f"qa_p_c{k}", [128, 512]) for k in range(3)]
        p_y = [ps(f"qa_p_y{u}", [128, 512]) for u in range(2)]
        p_o = ps("qa_p_o", [128, 512])
        s_w, s_xn, s_tr, s_xt, s_q, s_sq, s_sum, s_root, s_qn, s_prod, s_turn, s_part, s_mul, s_y, s_yn, s_ty, s_yt, s_o, s_x = (
            sem("qa_" + x) for x in ("s_w", "s_xn", "s_tr", "s_xt", "s_q", "s_sq", "s_sum", "s_root", "s_qn", "s_prod",
                                     "s_turn", "s_part", "s_mul", "s_y", "s_yn", "s_ty", "s_yt", "s_o", "s_x"))
        NC = H + 1
        heads = lambda x: x.rearrange("p (h f) -> p h f", h=H)

        with m.block() as block:
            @block.sync
            def _(sp):
                sp.dma_start(w_q[:, :, :], a["L1_mix_Wqkv"][:, 0:C].rearrange("(c p) n -> p c n", p=128)).then_inc(s_w, 16)
                sp.dma_start(b_q[:, :], a["L1_mix_bqkv"][0:C].rearrange("(o n) -> o n", o=1)).then_inc(s_w, 16)
                sp.dma_start(w_p[:, :, :], a["L1_mix_Wproj"].rearrange("(c p) n -> p c n", p=128)).then_inc(s_w, 16)
                sp.dma_start(b_p[:, :], a["L1_mix_bproj"].rearrange("(o n) -> o n", o=1)).then_inc(s_w, 16)
                sp.dma_start(temp[:, :], a["L1_mix_temperature"].rearrange("a h b c -> a (h b c)").broadcast_to((P, H))).then_inc(s_w, 16)

            @block.scalar
            def _(act):
                def front(n):
                    if not first(n):
                        act.wait_ge(s_tr, n)
                    act.activation(xn[:, :], m.x[:, n, :], ACT.Identity, scale=m.rstd[:, bass.ds(n, 1)],
                                   bias=m.nmr[:, bass.ds(n, 1)]).then_inc(s_xn, 1)
                    act.wait_ge(s_tr, n + 1)
                    act.copy(xt[:, :, :].rearrange("p c n -> p (c n)"), p_q[:, 0:2 * P]).then_inc(s_xt, 1)
                    act.wait_ge(s_q, n + 1)
                    act.activation(sq[:, :], p_q[0:P, 256:512], ACT.Square, scale=Q_SCALE).then_inc(s_sq, 1)

                def take_root(n):
                    act.wait_ge(s_sum, n + 1)
                    act.activation(root[:, :], root[:, :], ACT.Sqrt).then_inc(s_root, 1)

                front(0)
                take_root(0)

                def step(n, u, last):
                    for c in range(NC):
                        act.wait_ge(s_turn, n * NC + c + 1)
                        if not (first(n) and c < 3):
                            act.wait_ge(s_mul, n * NC + c - 2)
                        act.copy(part[c % 3][:, :, :].rearrange("p k n -> p (k n)"), p_c[c % 3][:, 0:4 * P]).then_inc(s_part, 1)
                        if c == 2 and not last:
                            front(n + 1)
                        if c == 5 and not last:
                            take_root(n + 1)
                    if not first(n):
                        turn_y(n - 1)

                def turn_y(n):
                    act.wait_ge(s_ty, n + 1)
                    act.copy(yt[:, :, :].rearrange("p c n -> p (c n)"), p_o[:, 0:2 * P]).then_inc(s_yt, 1)

                in_units_last(act, step)
                turn_y(NT - 1)

            @block.vector
            def _(dve):
                dve.wait_ge(s_w, 80)
                dve.tensor_scalar(temp[:, :], temp[:, :], Q_SCALE ** 2, None, ALU.mult)

                def square_sum(n):
                    dve.wait_ge(s_sq, n + 1)
                    dve.tensor_reduce(root[:, :], heads(sq[:, :]), AX.X, ALU.add).then_inc(s_sum, 1)

                def divide(n, u):
                    dve.wait_ge(s_y, n + 1)
                    if not first(n):
                        dve.wait_ge(s_ty, n)
                    v = p_y[u][0:P, 0:2 * HALF].rearrange("p (h v) -> p h v", h=H)
                    dve.reciprocal(z[:, :], v[:, :, 0])
                    dve.drain()
                    dve.tensor_tensor(heads(y[:, :]), v[:, :, 1:HB], z[:, :].unsqueeze(2).broadcast_to((P, H, D)),
                                      ALU.mult).then_inc(s_yn, 1)

                def add(n):
                    dve.wait_ge(s_o, n + 1)
                    dve.tensor_tensor(m.x[:, n, :], m.x[:, n, :], p_o[0:P, 256:512], ALU.add).then_inc(s_x, 1)

                square_sum(0)

                def step(n, u, last):
                    dve.wait_ge(s_root, n + 1)
                    if later(n):
                        dve.wait_ge(s_turn, (n - 1) * NC)
                    unit_rows(dve, root[:, :], heads(p_q[0:P, 256:512]), far[u][:, 1, :, :], q2[u], temp[:, :])
                    dve.drain().then_inc(s_qn, 1)
                    shifted_products(dve, far[u][:, 1, :, :], q2[u], prod[u], far[u][:, 0, :, :]).then_inc(s_prod, 1)
                    if not last:
                        square_sum(n + 1)
                    if not first(n):
                        divide(n - 1, 1 - u)
                    if later(n):
                        add(n - 2)

                in_units_last(dve, step)
                divide(NT - 1, (NT - 1) % 2)
                add(NT - 2)
                add(NT - 1)

            @block.tensor
            def _(pe):
                pe.wait_ge(s_w, 80)

                def front(n):
                    pe.wait_ge(s_xn, n + 1)
                    if not first(n):
                        pe.wait_ge(s_qn, n)
                    for c in range(2):
                        mm = pe.transpose(p_q[:, P * c:P * c + P], xn[:, 128 * c:128 * c + 128], m.ident[0:P, 0:P])
                    mm.then_inc(s_tr, 1)
                    pe.wait_ge(s_xt, n + 1)
                    for c in range(2):
                        pe.matmul(p_q[0:P, 256:512], xt[:, c, :], w_q[:, c, :], start=c == 0, stop=False)
                    pe.matmul(p_q[0:P, 256:512], m.ones[0:1, 0:P], b_q[0:1, :], start=False, stop=True).then_inc(s_q, 1)

                def turn(n, u, c):
                    if not (first(n) and c < 3):
                        pe.wait_ge(s_part, n * NC + c - 2)
                    for k in range(4):
                        if c == 0:
                            g = k % 2
                            rows = far[u][:, k // 2, 4 * g:4 * g + 4, :].rearrange("p h i -> p (h i)")
                        else:
                            rows = prod[u][:, c - 1, 4 * k:4 * k + 4, :].rearrange("p s i -> p (s i)")
                        mm = pe.transpose(p_c[c % 3][:, P * k:P * k + P], rows, m.ident[0:P, 0:P])
                    mm.then_inc(s_turn, 1)

                def multiply(n, u, c):
                    pe.wait_ge(s_part, n * NC + c + 1)
                    for k in range(4):
                        if c == 0:
                            g = k % 2
                            out, rhs = p_y[u][0:P, HALF * g:HALF * g + HALF], m_far[:, k // 2, g, :]
                        else:
                            out, rhs = p_y[u][0:P, HB * (c - 1):HB * c], m_near[:, 4 * (c - 1) + k, :]
                        mm = pe.matmul(out, part[c % 3][:, k, :], rhs, start=False, stop=False, skip_group_check=True)
                    mm.then_inc(s_mul, 1)

                def project(n):
                    pe.wait_ge(s_yn, n + 1)
                    if not first(n):
                        pe.wait_ge(s_x, n)
                    for c in range(2):
                        mm = pe.transpose(p_o[:, P * c:P * c + P], y[:, 128 * c:128 * c + 128], m.ident[0:P, 0:P])
                    mm.then_inc(s_ty, 1)
                    pe.wait_ge(s_yt, n + 1)
                    for c in range(2):
                        pe.matmul(p_o[0:P, 256:512], yt[:, c, :], w_p[:, c, :], start=c == 0, stop=False)
                    pe.matmul(p_o[0:P, 256:512], m.ones[0:1, 0:P], b_p[0:1, :], start=False, stop=True).then_inc(s_o, 1)

                front(0)

                def step(n, u, last):
                    pe.wait_ge(s_prod, n + 1)
                    if later(n):
                        pe.wait_ge(s_yn, n - 1)
                    pe.matmul(p_y[u][0:P, 0:2 * HALF], m.ones[0:1, 0:P], v_sum[0:1, :, :].rearrange("p g v -> p (g v)"),
                              start=True, stop=False, skip_group_check=True)
                    for c in range(NC):
                        turn(n, u, c)
                        if c == 3 and not last:
                            front(n + 1)
                        if c > 0:
                            multiply(n, u, c - 1)
                    multiply(n, u, NC - 1)
                    pe.drain().then_inc(s_y, 1)
                    if not first(n):
                        project(n - 1)

                in_units_last(pe, step)
                project(NT - 1)


def aggregate(nc, m, a, row_i, node_f, acc):
    with ExitStack() as ctx:
        sb, ps, sem = m.scope(nc, ctx)
        stage = [sb(f"ag_stage{u}", [128, G], I32) for u in range(4)]
        rows = [sb(f"ag_rows{u}", [128, G, C], F32) for u in range(2)]
        hot = [sb(f"ag_hot{u}", [128, G, P], F32) for u in range(2)]
        p_a = [ps(f"ag_p_a{k}", [128, 512]) for k in range(8)]
        s_gath = [sem(f"ag_s_gath{u}") for u in range(2)]
        s_stage, s_hot, s_agg, s_acc, s_zero = (sem("ag_" + x) for x in ("s_stage", "s_hot", "s_agg", "s_acc", "s_zero"))
        with m.block() as block:
            @block.gpsimd
            def _(pool):
                pool.tensor_copy(stage[0][:, :], row_i[:, 0:G]).then_inc(s_stage, 1)

                def step(n, u, last):
                    if later(n):
                        pool.wait_ge(s_agg, n * G - G)
                    pool.wait_ge(s_stage, n + 1)
                    pool.tensor_copy(stage[(u + 1) % 4][:, :], row_i[:, bass.ds((n + 1) * G, G)]).then_inc(s_stage, 1)
                    for g in range(G):
                        pool.indirect_dma_start(out=rows[u % 2][:, g, :], out_offset=None, in_=m.table1,
                                                in_offset=bass.IndirectOffsetOnAxis(ap=stage[u][:, g:g + 1], axis=0)
                                                ).then_inc(s_gath[u % 2], 16)

                in_groups(pool, step, 4)

            @block.vector
            def _(dve):
                dve.memset(acc[:, :, :], 0.0)
                dve.drain()

                def one_hot(n, u):
                    if later(n):
                        dve.wait_ge(s_agg, n * G - G)
                    dve.tensor_tensor(hot[u][:, :, :], m.count_p[:, :].unsqueeze(1).broadcast_to((128, G, P)),
                                      node_f[:, bass.ds(n * G, G)].unsqueeze(2).broadcast_to((128, G, P)),
                                      ALU.is_equal).then_inc(s_hot, 1)

                one_hot(0, 0)

                def step(n, u, last):
                    if not last:
                        one_hot(n + 1, 1 - u)
                    tiles = tiles_of(nc, mybir.EngineType.DVE, m.tile_src, n)
                    for g in range(G):
                        t = tiles[g]
                        if not (isinstance(n, int) and n == 0 and g == 0):
                            dve.wait_ge(s_acc, n * G + g)
                        dve.wait_ge(s_agg, n * G + g + 1)
                        row = acc[:, bass.ds(t, 1), :].rearrange("p o w -> p (o w)")
                        dve.tensor_tensor(row, row, p_a[4 * u + g % 4][0:P, 0:C], ALU.add).then_inc(s_acc, 1)

                in_groups(dve, step)

            @block.tensor
            def _(pe):
                def step(n, u, last):
                    pe.wait_ge(s_hot, n + 1)
                    pe.wait_ge(s_gath[u], rounds(n, u, 16 * G))
                    for g in range(G):
                        if g >= 4:
                            pe.wait_ge(s_acc, n * G + g - 3)
                        elif g == 0 and later(n):
                            pe.wait_ge(s_acc, n * G - G)
                        pe.matmul(p_a[4 * u + g % 4][0:P, 0:C], hot[u][:, g, :], rows[u][:, g, :],
                                  start=True, stop=True).then_inc(s_agg, 1)

                in_groups(pe, step)


def relational_add(nc, m, a, acc):
    with ExitStack() as ctx:
        sb, ps, sem = m.scope(nc, ctx)
        bias = sb("ra_bias", [P, C], F32)
        y = [sb(f"ra_y{u}", [P, C], F32) for u in range(2)]
        s_b, s_x = sem("ra_s_b"), sem("ra_s_x")
        with m.block() as block:
            @block.sync
            def _(sp):
                sp.dma_start(bias[:, :], a["L1_gnn_bias"].rearrange("(o c) -> o c", o=1).broadcast_to((P, C))).then_inc(s_b, 16)

            @block.vector
            def _(dve):
                dve.wait_ge(s_b, 16)

                def step(n, u):
                    if later(n):
                        dve.wait_ge(s_x, n - 1)
                    dve.tensor_tensor(y[u][:, :], acc[:, bass.ds(n, 1), :].rearrange("p o c -> p (o c)"), bias[:, :], ALU.add)
                    dve.drain()
                    dve.scalar_tensor_tensor(out=m.x[:, n, :], in0=y[u][:, :], scalar=0.0, in1=m.x[:, n, :],
                                             op0=ALU.max, op1=ALU.add).then_inc(s_x, 1)

                in_units(dve, step, NT)


MT = 4
FH = 512
NE = 8


def experts(nc, m, a, out):
    with ExitStack() as ctx:
        sb, ps, sem = m.scope(nc, ctx)
        w1 = sb("ex_w1", [128, 2, NE, FH], F32)
        w2 = sb("ex_w2", [128, NE, 4, C], F32)
        b1 = sb("ex_b1", [128, NE * 4], F32)
        b2 = sb("ex_b2", [NE, C], F32)
        w_g = sb("ex_w_g", [128, 2, NE], F32)
        b_g = sb("ex_b_g", [1, NE], F32)
        xn = sb("ex_xn", [P, MT, C], F32)
        xt = sb("ex_xt", [128, 2, MT, P], F32)
        ht = [sb(f"ex_ht{u}", [128, 4, MT * P], F32) for u in range(2)]
        y = sb("ex_y", [P, MT, C], F32)
        prob = sb("ex_prob", [P, MT, NE], F32)
        col = sb("ex_col", [P, MT], F32)
        over = sb("ex_over", [P, MT, NE, NE], F32)
        same = sb("ex_same", [P, MT, NE, NE], F32)
        before = sb("ex_before", [P, NE, NE], F32)
        cw = sb("ex_cw", [P, MT, NE], F32)
        cwt = sb("ex_cwt", [NE, MT, P], F32)
        p_t = [ps(f"ex_p_t{k}", [128, 512]) for k in range(2)]
        p_h = [ps(f"ex_p_h{k}", [128, 512]) for k in range(4)]
        p_y = [ps(f"ex_p_y{k}", [128, 512]) for k in range(2)]
        s_w, s_tri, s_xn, s_tr, s_xt, s_gate, s_sub, s_exp, s_cw, s_cwt_p, s_cwt, s_b, s_b_add, s_h, s_gelu, s_y, s_add, s_out = (
            sem("ex_" + x) for x in ("s_w", "s_tri", "s_xn", "s_tr", "s_xt", "s_gate", "s_sub", "s_exp", "s_cw",
                                     "s_cwt_p", "s_cwt", "s_b", "s_b_add", "s_h", "s_gelu", "s_y", "s_add", "s_out"))
        steps = NT // MT

        def in_steps(eng, body):
            body(0, MT, MT)
            with eng.Fori(1, steps - 1) as i:
                body(i, MT, MT)
            body(steps - 1, MT, NT - steps * MT)
            body(steps, NT - steps * MT, 0)

        with m.block() as block:
            @block.sync
            def _(sp):
                for c in range(2):
                    sp.dma_start(w1[:, c, :, :], a["L1_ffn_W1"][:, 128 * c:128 * c + 128, :].rearrange("e p n -> p e n")).then_inc(s_w, 16)
                for k in range(4):
                    sp.dma_start(w2[:, :, k, :], a["L1_ffn_W2"][:, 128 * k:128 * k + 128, :].rearrange("e p n -> p e n")).then_inc(s_w, 16)
                sp.dma_start(b1[:, :], a["L1_ffn_b1"].rearrange("e (k p) -> p (e k)", p=128), allow_slow_non_contiguous=True).then_inc(s_w, 16)
                sp.dma_start(b2[:, :], a["L1_ffn_b2"]).then_inc(s_w, 16)
                sp.dma_start(w_g[:, :, :], a["L1_ffn_gate_w"].rearrange("(c p) e -> p c e", p=128)).then_inc(s_w, 16)
                sp.dma_start(b_g[:, :], a["L1_ffn_gate_b"].rearrange("(o e) -> o e", o=1)).then_inc(s_w, 16)

                def step(i, k, k_next):
                    sp.wait_ge(s_add, i * NE + NE)
                    sp.dma_start(out.rearrange("(t p) c -> p t c", p=P)[:, bass.ds(i * MT, k), :],
                                 y[:, 0:k, :]).then_inc(s_out, 16)

                in_steps(sp, step)
                sp.wait_ge(s_out, (steps + 1) * 16)

            @block.scalar
            def _(act):
                act.wait_ge(s_w, 160)

                def norm(i, k):
                    if not first(i):
                        act.wait_ge(s_tr, i * 2)
                    for j in range(k):
                        n = i * MT + j
                        ins = act.activation(xn[:, j, :], m.x[:, n, :], ACT.Identity, scale=m.rstd[:, bass.ds(n, 1)],
                                             bias=m.nmr[:, bass.ds(n, 1)])
                    ins.then_inc(s_xn, 1)

                def copy_xt(i, k):
                    if not first(i):
                        act.wait_ge(s_h, i * NE * 4)
                    for c in range(2):
                        act.wait_ge(s_tr, i * 2 + c + 1)
                        act.copy(xt[:, c, 0:k, :].rearrange("p t n -> p (t n)"), p_t[c][:, 0:k * P]).then_inc(s_xt, 1)

                norm(0, MT)
                copy_xt(0, MT)

                def step(i, k, k_next):
                    act.wait_ge(s_sub, i + 1)
                    act.activation(prob[:, 0:k, :], prob[:, 0:k, :], ACT.Exp).then_inc(s_exp, 1)
                    for e in range(NE):
                        if not (first(i) and e < 2):
                            act.wait_ge(s_y, i * NE + e - 1)
                        for q in range(4):
                            act.wait_ge(s_h, (i * NE + e) * 4 + q + 1)
                            act.activation(ht[e % 2][:, q, 0:k * P], p_h[q][:, 0:k * P], ACT.Gelu,
                                           bias=b1[:, 4 * e + q:4 * e + q + 1]).then_inc(s_gelu, 1)
                        if e == NE // 2 and k_next:
                            norm(i + 1, k_next)
                    if k_next:
                        copy_xt(i + 1, k_next)

                in_steps(act, step)

            @block.gpsimd
            def _(pool):
                pool.affine_select(out=before[:, :, :], in_=m.ones[0:P, 0:NE * NE].rearrange("p (e j) -> p e j", e=NE),
                                   compare_op=ALU.is_gt, fill=0.0, base=0, pattern=[[1, NE], [-1, NE]],
                                   channel_multiplier=0).then_inc(s_tri, 1)

            @block.vector
            def _(dve):
                dve.wait_ge(s_tri, 1)

                def step(i, k, k_next):
                    wide = lambda x: x.unsqueeze(2).broadcast_to((P, k, NE))
                    p, c = prob[:, 0:k, :], col[:, 0:k]
                    dve.wait_ge(s_gate, i + 1)
                    gate = p_t[0][0:P, 0:k * NE].rearrange("p (t e) -> p t e", e=NE)
                    dve.tensor_reduce(c, gate, AX.X, ALU.max)
                    dve.drain()
                    dve.tensor_tensor(p, gate, wide(c), ALU.subtract).then_inc(s_sub, 1)
                    dve.wait_ge(s_exp, i + 1)
                    dve.tensor_reduce(c, p, AX.X, ALU.add)
                    dve.drain()
                    dve.reciprocal(c, c)
                    dve.drain()
                    dve.tensor_tensor(p, p, wide(c), ALU.mult)
                    dve.drain()
                    own = p.unsqueeze(3).broadcast_to((P, k, NE, NE))
                    other = p.unsqueeze(2).broadcast_to((P, k, NE, NE))
                    dve.tensor_tensor(over[:, 0:k, :, :], other, own, ALU.is_gt)
                    dve.tensor_tensor(same[:, 0:k, :, :], other, own, ALU.is_equal)
                    dve.drain()
                    dve.tensor_tensor(same[:, 0:k, :, :], same[:, 0:k, :, :],
                                      before[:, :, :].unsqueeze(1).broadcast_to((P, k, NE, NE)), ALU.mult)
                    dve.drain()
                    dve.tensor_tensor(over[:, 0:k, :, :], over[:, 0:k, :, :], same[:, 0:k, :, :], ALU.add)
                    dve.drain()
                    dve.tensor_reduce(cw[:, 0:k, :], over[:, 0:k, :, :], AX.X, ALU.add)
                    dve.drain()
                    dve.scalar_tensor_tensor(out=cw[:, 0:k, :], in0=cw[:, 0:k, :], scalar=2.0, in1=p,
                                             op0=ALU.is_lt, op1=ALU.mult).then_inc(s_cw, 1)
                    dve.wait_ge(s_cwt_p, i + 1)
                    dve.tensor_copy(cwt[:, 0:k, :].rearrange("e t n -> e (t n)"), p_t[1][0:NE, 0:k * P]).then_inc(s_cwt, 1)
                    if not first(i):
                        dve.wait_ge(s_out, i * 16)
                    dve.wait_ge(s_b, i + 1)
                    for j in range(0, k, 2):
                        dve.tensor_tensor(y[:, j:j + 2, :], m.x[:, bass.ds(i * MT + j, 2), :],
                                          p_y[j // 2][0:P, :].rearrange("p (t c) -> p t c", t=2), ALU.add)
                    dve.drain().then_inc(s_b_add, 1)
                    for e in range(NE):
                        dve.wait_ge(s_y, i * NE + e + 1)
                        for j in range(k):
                            dve.scalar_tensor_tensor(out=y[:, j, :], in0=p_y[j // 2][0:P, C * (j % 2):C * (j % 2) + C],
                                                     scalar=cw[:, j, e:e + 1], in1=y[:, j, :], op0=ALU.mult, op1=ALU.add)
                        dve.drain().then_inc(s_add, 1)

                in_steps(dve, step)

            @block.tensor
            def _(pe):
                pe.wait_ge(s_w, 160)

                def hidden(i, k, e):
                    for q in range(4):
                        if not (first(i) and e == 0):
                            pe.wait_ge(s_gelu, (i * NE + e) * 4 + q - 3)
                        for c in range(2):
                            mm = pe.matmul(p_h[q][:, 0:k * P], w1[:, c, e, 128 * q:128 * q + 128],
                                           xt[:, c, 0:k, :].rearrange("p t n -> p (t n)"), start=c == 0, stop=c == 1)
                        mm.then_inc(s_h, 1)

                def turn(i, k):
                    pe.wait_ge(s_xn, i + 1)
                    if not first(i):
                        pe.wait_ge(s_sub, i)
                        pe.wait_ge(s_cwt, i)
                    for c in range(2):
                        for j in range(k):
                            mm = pe.transpose(p_t[c][:, P * j:P * j + P], xn[:, j, 128 * c:128 * c + 128], m.ident[0:P, 0:P])
                        mm.then_inc(s_tr, 1)

                turn(0, MT)

                def step(i, k, k_next):
                    pe.wait_ge(s_xt, i * 2 + 2)
                    for j in range(k):
                        for c in range(2):
                            pe.matmul(p_t[0][0:P, NE * j:NE * j + NE], xt[:, c, j, :], w_g[:, c, :], start=c == 0, stop=False)
                        mm = pe.matmul(p_t[0][0:P, NE * j:NE * j + NE], m.ones[0:1, 0:P], b_g[0:1, :], start=False, stop=True)
                    mm.then_inc(s_gate, 1)
                    hidden(i, k, 0)
                    pe.wait_ge(s_cw, i + 1)
                    for j in range(k):
                        mm = pe.transpose(p_t[1][0:NE, P * j:P * j + P], cw[:, j, :], m.ident[0:P, 0:P])
                    mm.then_inc(s_cwt_p, 1)
                    pe.wait_ge(s_cwt, i + 1)
                    if not first(i):
                        pe.wait_ge(s_add, i * NE)
                    for j in range(k):
                        mm = pe.matmul(p_y[j // 2][0:P, C * (j % 2):C * (j % 2) + C], cwt[:, j, :], b2[:, :], start=True, stop=True)
                    mm.then_inc(s_b, 1)
                    for e in range(NE):
                        if e + 1 < NE:
                            hidden(i, k, e + 1)
                        if e == NE - 2 and k_next:
                            turn(i + 1, k_next)
                        if e == 0:
                            pe.wait_ge(s_b_add, i + 1)
                        else:
                            pe.wait_ge(s_add, i * NE + e)
                        pe.wait_ge(s_gelu, (i * NE + e) * 4 + 4)
                        for j in range(k):
                            for q in range(4):
                                mm = pe.matmul(p_y[j // 2][0:P, C * (j % 2):C * (j % 2) + C], ht[e % 2][:, q, P * j:P * j + P],
                                               w2[:, e, q, :], start=q == 0, stop=q == 3)
                        mm.then_inc(s_y, 1)

                in_steps(pe, step)


def program(nc, a, out):
    with ExitStack() as ctx:
        m = Shared()
        m.sb = lambda name, shape, dt: ctx.enter_context(nc.sbuf_tensor(name, shape, dt))
        m.sem = lambda name: ctx.enter_context(nc.semaphore(name))
        m.block = nc.Block
        m.blocks = 0

        def next_block():
            m.blocks += 1
            return m.blocks

        m.next_block = next_block

        spent = []

        def phase_semaphore(name):
            spent.append(nc.alloc_semaphore(name))
            return spent[-1]

        def clear_semaphores():
            nc.all_engine_barrier()
            nc.clear_and_free_semaphores(spent)
            nc.all_engine_barrier()
            spent.clear()

        def scope(nc, inner):
            return (lambda name, shape, dt: inner.enter_context(nc.sbuf_tensor(name, shape, dt)),
                    lambda name, shape: inner.enter_context(nc.psum_tensor(name, shape, F32)),
                    phase_semaphore)

        m.scope = scope
        m.table0 = nc.dram_tensor("table0", (N + 1, TW), F32).ap()
        m.skip_rows = nc.dram_tensor("skip_rows", (N, C), F32).ap()
        m.table1 = nc.dram_tensor("table1", (R * N, C), F32).ap()
        slots_dst = nc.dram_tensor("slots_dst", (LANES * CH, 1), I32).ap()
        slots_src = nc.dram_tensor("slots_src", (LANES * CH, 1), I32).ap()
        constants(nc, m)
        load_inputs(nc, m, a)
        m.mean = m.sb("mean", [P, NT], F32)
        m.rstd = m.sb("rstd", [P, NT], F32)
        m.nmr = m.sb("nmr", [P, NT], F32)
        m.score = m.sb("score", [P, NT, 2 * H], F32)
        m.kv_sum = m.sb("kv_sum", [128, 258], F32)
        m.tmp = m.sb("tmp", [P, NT * 8], F32)
        m.tile_dst = m.sb("tile_dst", [1, CH], I16)
        m.tile_src = m.sb("tile_src", [1, CH], I16)
        pi_src = m.sb("pi_src", [P, EC, 2], I32)
        stage = [m.sb(f"scatter_stage{u}", [P, SG, 2], I32) for u in range(2)]
        with ExitStack() as dst_only:
            hold = lambda name, shape, dt: dst_only.enter_context(nc.sbuf_tensor(name, shape, dt))
            m.chunk_i = hold("chunk_i", [NT, CH], I32)
            pi_dst = hold("pi_dst", [P, EC, 2], I32)
            fill_slots(nc, m, [slots_dst, slots_src])
            rank_edges(nc, m, a["dst"], [a["src"]], pi_dst, m.tile_dst, "dst")
            job = scatter_job(m, pi_dst, slots_dst, stage, "dst")
            t = Together()
            m.block = lambda: t
            row_statistics(nc, m, m.x, m.mean, m.rstd, m.tmp, "l0")
            shift_of(nc, m, m.mean, m.rstd, m.nmr)
            project_l0(nc, m, a)
            rank_edges(nc, m, a["src"], [a["edge_type_8"], a["dst"]], pi_src, m.tile_src, "src")
            msg = hold("msg", [P, NT, C], F32)
            mean, rstd, nmr = (hold(x, [P, NT], F32) for x in ("msg_mean", "msg_rstd", "msg_nmr"))
            mix_query(nc, m, a, msg)
            row_statistics(nc, m, msg, mean, rstd, m.tmp, "msg")
            shift_of(nc, m, mean, rstd, nmr)
            mix_mlp(nc, m, a, msg, rstd, nmr)
            row_statistics(nc, m, msg, mean, rstd, m.tmp, "h")
            shift_of(nc, m, mean, rstd, nmr)
            mix_add(nc, m, a, msg, rstd, nmr)
            t.run(nc, m, job)
            m.block = nc.Block
            clear_semaphores()
        with ExitStack() as attention:
            hold = lambda name, shape, dt: attention.enter_context(nc.sbuf_tensor(name, shape, dt))
            acc = hold("acc", [P, NT, TW], F32)
            smax = hold("smax", [128, G * H], F32)
            with ExitStack() as sorted_edges:
                row_i = sorted_edges.enter_context(nc.sbuf_tensor("row_i", [LANES, CH + G], I32))
                node_f = sorted_edges.enter_context(nc.sbuf_tensor("node_f", [LANES, CH], F32))
                load_slots(nc, m, slots_dst, row_i, node_f, "dst")
                score_bounds(nc, m, acc, smax)
                attend(nc, m, row_i, node_f, acc, smax)
            z = hold("z", [P, NT, H], F32)
            attention_sums(nc, m, acc, smax, z)
            job = scatter_job(m, pi_src, slots_src, stage, "src")
            t = Together()
            m.block = lambda: t
            attention_add(nc, m, a, acc, z)
        with ExitStack() as slices:
            hold = lambda name, shape, dt: slices.enter_context(nc.sbuf_tensor(name, shape, dt))
            row_statistics(nc, m, m.x, m.mean, m.rstd, m.tmp, "ffn")
            shift_of(nc, m, m.mean, m.rstd, m.nmr)
            swt = hold("swt", [128, NT, 4, P], F32)
            with ExitStack() as sums:
                sx = sums.enter_context(nc.sbuf_tensor("sx", [128, 4, C + 1], F32))
                with ExitStack() as logits:
                    w_log = logits.enter_context(nc.sbuf_tensor("w_log", [128, 2, H * SL], F32))
                    b_log = logits.enter_context(nc.sbuf_tensor("b_log", [1, H * SL], F32))
                    slice_logits_weights(nc, m, a, w_log, b_log)
                    slice_weights(nc, m, w_log, b_log, swt, sx)
                w_back = sums.enter_context(nc.sbuf_tensor("w_back", [128, 4, C], F32))
                slice_attention(nc, m, a, sx, w_back)
                slice_add(nc, m, a, swt, w_back)
            row_statistics(nc, m, m.x, m.mean, m.rstd, m.tmp, "l1")
            shift_of(nc, m, m.mean, m.rstd, m.nmr)
        with ExitStack() as quadratic:
            hold = lambda name, shape, dt: quadratic.enter_context(nc.sbuf_tensor(name, shape, dt))
            relation_table(nc, m, a)
            m_near = hold("m_near", [128, 4 * H, HB], F32)
            m_far = hold("m_far", [128, 2, 2, HALF], F32)
            v_sum = hold("v_sum", [1, 2, HALF], F32)
            moments(nc, m, a, m_near, m_far, v_sum)
            quadratic_attention(nc, m, a, m_near, m_far, v_sum)
        t.run(nc, m, job)
        m.block = nc.Block
        clear_semaphores()
        with ExitStack() as relational:
            hold = lambda name, shape, dt: relational.enter_context(nc.sbuf_tensor(name, shape, dt))
            row_i = hold("row_i1", [LANES, CH + G], I32)
            node_f = hold("node_f1", [LANES, CH], F32)
            acc = hold("acc1", [P, NT, C], F32)
            load_slots(nc, m, slots_src, row_i, node_f, "src")
            aggregate(nc, m, a, row_i, node_f, acc)
            relational_add(nc, m, a, acc)
        row_statistics(nc, m, m.x, m.mean, m.rstd, m.tmp, "moe")
        shift_of(nc, m, m.mean, m.rstd, m.nmr)
        experts(nc, m, a, out)


def shift_of(nc, m, mean, rstd, nmr):
    with m.block() as block:
        @block.vector
        def _(dve):
            dve.scalar_tensor_tensor(out=nmr[:, :], in0=mean[:, :], scalar=-1.0, in1=rstd[:, :],
                                     op0=ALU.mult, op1=ALU.mult)


_INS = ['x', 'src', 'dst', 'edge_type_8', 'L0_gnn_Wp', 'L0_gnn_a_src', 'L0_gnn_a_trg', 'L0_gnn_Wskip',
        'L0_gnn_bias', 'L0_mix_Wq', 'L0_mix_Wk', 'L0_mix_Wv', 'L0_mix_Wm', 'L0_mix_W1', 'L0_mix_W2', 'L0_mix_g1',
        'L0_mix_b1', 'L0_mix_g2', 'L0_mix_b2', 'L0_ffn_W_fx', 'L0_ffn_b_fx', 'L0_ffn_W_x', 'L0_ffn_b_x',
        'L0_ffn_W_slice', 'L0_ffn_b_slice', 'L0_ffn_W_q', 'L0_ffn_W_k', 'L0_ffn_W_v', 'L0_ffn_W_out',
        'L0_ffn_b_out', 'L0_ffn_temperature', 'L1_gnn_weight', 'L1_gnn_bias', 'L1_mix_Wqkv', 'L1_mix_bqkv',
        'L1_mix_Wproj', 'L1_mix_bproj', 'L1_mix_temperature', 'L1_ffn_gate_w', 'L1_ffn_gate_b', 'L1_ffn_W1',
        'L1_ffn_b1', 'L1_ffn_W2', 'L1_ffn_b2']
_TRANSPOSED = ('L0_gnn_Wp', 'L0_gnn_Wskip', 'L1_mix_Wqkv', 'L1_mix_Wproj')


def kernel(**inputs):
    import numpy as _np
    import concourse.bacc as _bacc
    from concourse import mybir as _mybir
    from concourse.bass_utils import run_bass_kernel_spmd as _run

    nc = _bacc.Bacc("TRN2", target_bir_lowering=False, num_devices=1)
    arrays, aps = {}, {}
    for name in _INS:
        v = _np.asarray(inputs[name])
        v = _np.ascontiguousarray(v.T if name in _TRANSPOSED else v)
        arrays[f"in_{name}"] = v
        aps[name] = nc.dram_tensor(f"in_{name}", v.shape, _mybir.dt.from_np(v.dtype), kind="ExternalInput").ap()
    out = nc.dram_tensor("out_x", (N, C), F32, kind="ExternalOutput").ap()
    program(nc, aps, out)
    r = _run(nc, [arrays], core_ids=[0])
    return r.results[0]["out_x"]
```
